# Optimizing a Trainium2 kernel written in Bass

```python
import numpy as np
import jax
import jax.numpy as jnp

def _softmax(x, axis=-1):
    return jax.nn.softmax(x, axis=axis)

def _gelu(x):
    return jax.nn.gelu(x, approximate=True)

def _silu(x):
    return jax.nn.silu(x)

def _sigmoid(x):
    return jax.nn.sigmoid(x)

def _layernorm(x, axis=-1, eps=1e-05):
    m = jnp.mean(x, axis=axis, keepdims=True)
    v = jnp.var(x, axis=axis, keepdims=True)
    return (x - m) / jnp.sqrt(v + eps)

def _scatter_add(tgt, idx, src, axis=0):
    return tgt.at[idx].add(src)

def _segment_sum(src, seg, n):
    return jax.ops.segment_sum(src, seg, n)
kernel_name = 'mk_prb_d1_jaxref_r4_f24f47'

def setup_inputs(seed: int=0):
    np.random.seed(seed)
    _w = jnp.asarray

    def _L0_attn_setup():
        import jax, jax.numpy as jnp
        import numpy as np
        B, T, D, H = (2, 512, 256, 16)
        Dh = D // H

        def _rope(q, k):
            t = q.shape[2]
            dh = q.shape[3]
            inv_freq = 1.0 / 10000.0 ** (jnp.arange(0, dh, 2, dtype=jnp.float32) / dh)
            pos = jnp.arange(t, dtype=jnp.float32)
            freqs = pos[:, None] * inv_freq[None, :]
            sin = jnp.sin(freqs)[None, None]
            cos = jnp.cos(freqs)[None, None]

            def rot(x):
                xe, xo = (x[..., ::2], x[..., 1::2])
                re = xe * cos - xo * sin
                ro = xe * sin + xo * cos
                return jnp.stack([re, ro], axis=-1).reshape(x.shape)
            return (rot(q), rot(k))
        key = jax.random.key(seed)
        k1, k2, k3 = jax.random.split(key, 3)
        s = 1.0 / np.sqrt(D)
        return {'x': jax.random.normal(k1, (B, T, D), dtype=jnp.float32), 'w_qkv': jax.random.normal(k2, (3 * D, D), dtype=jnp.float32) * s, 'b_qkv': jnp.zeros((3 * D,), dtype=jnp.float32), 'w_out': jax.random.normal(k3, (D, D), dtype=jnp.float32) * s, 'b_out': jnp.zeros((D,), dtype=jnp.float32)}
    _L0_attn_in = _L0_attn_setup()

    def _L0_ffn_setup():
        import jax, jax.numpy as jnp
        import numpy as np
        B, S, IN, OUT, E, R = (8, 1024, 256, 256, 8, 8)
        LORA_ALPHA = 16
        SCALING = LORA_ALPHA / R
        key = jax.random.key(seed)
        k = jax.random.split(key, 6)
        x = jax.random.normal(k[0], (B, S, IN), dtype=jnp.float32)
        base_w = jax.random.normal(k[1], (OUT, IN), dtype=jnp.float32) * 0.02
        base_b = jnp.zeros((OUT,), dtype=jnp.float32)
        lora_A = jax.random.normal(k[2], (IN, R), dtype=jnp.float32) * 0.02
        lora_B = jax.random.normal(k[3], (E, R, OUT), dtype=jnp.float32) * 0.02
        router_w = jax.random.normal(k[4], (E, IN), dtype=jnp.float32) * 0.02
        router_b = jnp.zeros((E,), dtype=jnp.float32)
        return {'x': x, 'base_w': base_w, 'base_b': base_b, 'lora_A': lora_A, 'lora_B': lora_B, 'router_w': router_w, 'router_b': router_b}
    _L0_ffn_in = _L0_ffn_setup()
    _d = {'L0_attn_x': _L0_attn_in['x'], 'L0_attn_w_qkv': _L0_attn_in['w_qkv'], 'L0_attn_b_qkv': _L0_attn_in['b_qkv'], 'L0_attn_w_out': _L0_attn_in['w_out'], 'L0_attn_b_out': _L0_attn_in['b_out'], 'L0_ffn_base_w': _L0_ffn_in['base_w'], 'L0_ffn_base_b': _L0_ffn_in['base_b'], 'L0_ffn_lora_A': _L0_ffn_in['lora_A'], 'L0_ffn_lora_B': _L0_ffn_in['lora_B'], 'L0_ffn_router_w': _L0_ffn_in['router_w'], 'L0_ffn_router_b': _L0_ffn_in['router_b']}
    _x0 = _d['L0_attn_x']
    _d['L0_attn_x'] = jax.random.normal(jax.random.fold_in(jax.random.key(seed), 1), (16, 1024, 256), dtype=_x0.dtype)
    del _x0
    return _d

def reference(L0_attn_x, L0_attn_w_qkv, L0_attn_b_qkv, L0_attn_w_out, L0_attn_b_out, L0_ffn_base_w, L0_ffn_base_b, L0_ffn_lora_A, L0_ffn_lora_B, L0_ffn_router_w, L0_ffn_router_b):

    def _L0_attn_ref(x, w_qkv, b_qkv, w_out, b_out):
        import jax, jax.numpy as jnp
        import numpy as np
        B, T, D, H = (2, 512, 256, 16)
        Dh = D // H

        def _rope(q, k):
            t = q.shape[2]
            dh = q.shape[3]
            inv_freq = 1.0 / 10000.0 ** (jnp.arange(0, dh, 2, dtype=jnp.float32) / dh)
            pos = jnp.arange(t, dtype=jnp.float32)
            freqs = pos[:, None] * inv_freq[None, :]
            sin = jnp.sin(freqs)[None, None]
            cos = jnp.cos(freqs)[None, None]

            def rot(x):
                xe, xo = (x[..., ::2], x[..., 1::2])
                re = xe * cos - xo * sin
                ro = xe * sin + xo * cos
                return jnp.stack([re, ro], axis=-1).reshape(x.shape)
            return (rot(q), rot(k))
        b, t, d = x.shape
        qkv = x @ w_qkv.T + b_qkv
        q, k, v = jnp.split(qkv, 3, axis=-1)
        q = q.reshape(b, t, H, Dh).transpose(0, 2, 1, 3)
        k = k.reshape(b, t, H, Dh).transpose(0, 2, 1, 3)
        v = v.reshape(b, t, H, Dh).transpose(0, 2, 1, 3)
        q, k = _rope(q, k)
        scores = jnp.einsum('bhtd,bhsd->bhts', q, k) / jnp.sqrt(jnp.float32(Dh))
        causal = jnp.tril(jnp.ones((t, t), dtype=bool))[None, None]
        scores = jnp.where(causal, scores, -jnp.inf)
        probs = jax.nn.softmax(scores, axis=-1)
        out = jnp.einsum('bhts,bhsd->bhtd', probs, v)
        out = out.transpose(0, 2, 1, 3).reshape(b, t, d)
        return out @ w_out.T + b_out

    def _L0_ffn_ref(x, base_w, base_b, lora_A, lora_B, router_w, router_b):
        import jax, jax.numpy as jnp
        import numpy as np
        B, S, IN, OUT, E, R = (8, 1024, 256, 256, 8, 8)
        LORA_ALPHA = 16
        SCALING = LORA_ALPHA / R
        result = jnp.einsum('bsd,od->bso', x, base_w) + base_b
        logits = jnp.einsum('bsd,ed->bse', x, router_w) + router_b
        gating = jax.nn.softmax(logits, axis=-1).astype(jnp.bfloat16)
        mid = jnp.einsum('bsd,dr->bsr', x, lora_A)
        lora_out = jnp.einsum('bsr,erd,bse->bsd', mid, lora_B, gating.astype(jnp.float32))
        return result + lora_out * SCALING
    x = L0_attn_x
    xn = _layernorm(x, axis=-1)
    x = x + _L0_attn_ref(xn, L0_attn_w_qkv, L0_attn_b_qkv, L0_attn_w_out, L0_attn_b_out) + _L0_ffn_ref(xn, L0_ffn_base_w, L0_ffn_base_b, L0_ffn_lora_A, L0_ffn_lora_B, L0_ffn_router_w, L0_ffn_router_b)
    return x

_drawn_inputs = setup_inputs


def setup_inputs(seed=0):
    import zlib

    import numpy as np

    out = dict(_drawn_inputs(seed))
    spreads = {'L0_attn_b_qkv': (0.0, 0.1),
     'L0_attn_b_out': (0.0, 0.1),
     'L0_ffn_base_b': (0.0, 0.1),
     'L0_ffn_router_b': (0.0, 0.8)}
    factors = {'L0_ffn_lora_A': 4.522, 'L0_ffn_lora_B': 4.584, 'L0_ffn_router_w': 8.0}
    for name, (base, spread) in spreads.items():
        noise = np.random.default_rng([zlib.crc32(name.encode()), seed]).standard_normal(out[name].shape)
        drawn = base * np.exp(spread * noise) if base else spread * noise
        out[name] = jnp.asarray(drawn.astype(out[name].dtype))
    for name, factor in factors.items():
        out[name] = (out[name] * factor).astype(out[name].dtype)
    return out
```

```python
from contextlib import ExitStack

import concourse.bass as bass
from concourse import mybir

B, T, D, H, DH = 16, 1024, 256, 16, 16
E, R = 8, 8
SCALING = 2.0
EPS = 1e-5
SCORE_SCALE = DH ** -0.5
P = 128
BLK = T // P
KD = D // P
HALF = T // 2
QH = 4
QUADS = H // QH
VC = DH + 1
NML = R + E
PARTS = 3
STACK = 6 * DH
MROWS = STACK + PARTS
Q_PART = (0, 0, 1, 0, 1, 2)
K_PART = (0, 1, 0, 2, 1, 0)
MASKED = -1e30

REGIONS = []
PV_UNITS = []
for _half in range(2):
    for _kind, _j in [("A", j) for j in range(4 * _half + 1)] + [("B", 4 * _half + 1), ("C", 4 * _half + 2)]:
        _n = 1 if _kind == "C" else 2
        PV_UNITS.append((_half, _kind, _j, list(range(len(REGIONS), len(REGIONS) + _n))))
        REGIONS += [(_kind, _half, _j, 2 * a) for a in range(_n)]
NREG = len(REGIONS)
SLOTS = NREG * QUADS
MASK_REGIONS = [r for r, (kind, half, j, _) in enumerate(REGIONS) if j >= 4 * half]
HALF_END = [max(u[3][-1] for u in PV_UNITS if u[0] == h) for h in range(2)]
EXP_RING, PT_RING, LAG = 2, 6, 3

MAX_BANKS = []
for _i in range(BLK):
    _c0 = min(_i + 1, 4) * P
    _n = min(QH, HALF // _c0)
    MAX_BANKS += [(_i, 0, 0, _c0, list(range(a, a + _n))) for a in range(0, QH, _n)]
    if _i >= 4:
        _c1 = (_i - 3) * P
        _n = min(QH, HALF // _c1)
        MAX_BANKS += [(_i, 1, HALF, _c1, list(range(a, a + _n))) for a in range(0, QH, _n)]
NMAX = len(MAX_BANKS)
MAX_PER_SLOT = 3
MT_SLOT = 14
assert MAX_PER_SLOT * (MT_SLOT - 1) >= NMAX and NMAX % 2 == 0 and SLOTS % PT_RING == 0

TASKS = sorted(
    [(2, "stack3", 3)]
    + [(11 + c, "O", c) for c in range(4)]
    + [(15, "load_x", 0), (18, "stats", 0)]
    + [(19 + c, "T", c) for c in range(4)]
    + [(24 + 5 * (u // 2) + u % 2, "QK", u) for u in range(8)]
    + [(s, "V", i) for i, s in enumerate((23, 27, 28, 31, 33, 36, 38, 43))]
    + [(47, "stack", 0), (49, "stack", 1), (57, "stack", 2)]
    + [(44, "gate", 0), (52, "GT", 0)]
    + [(54 + 2 * c, "F", c) for c in range(4)]
)
BANK_KINDS = ("O", "T", "QK", "V", "GT", "F", "MT")
MTS = [(18 * g + MT_SLOT, "MT", g) for g in range(QUADS)]
BANK_ORDER = [(k, i) for s, k, i in sorted(TASKS + MTS, key=lambda x: (x[0], x[1] == "MT")) if k in BANK_KINDS]
NBANK = len(BANK_ORDER)
LAST_ORDER = [("O", c) for c in range(4)] + [("MT", g) for g in range(QUADS - 1)]
assert BANK_ORDER[:4] == LAST_ORDER[:4]
FIRST_ORDER = [("T", c) for c in range(4)] + [("QK", u) for u in range(8)] + [("V", i) for i in range(BLK)]
FIRST_ORDER += [("GT", 0)] + [("F", c) for c in range(4)] + [("MT", -1)]
NFIRST = len(FIRST_ORDER)
END_BASE = NFIRST - 4 + NBANK * (B - 1) + len(LAST_ORDER)


def attention_ffn_block(nc, x_in, wqk_in, bqk_in, wv_in, bv_in, base_in, wout_in, lora_in, bo_in, bb_in, cos_in, sin_in, out):
    f32, bf16 = mybir.dt.float32, mybir.dt.bfloat16
    ALU, ACT, AX = mybir.AluOpType, mybir.ActivationFunctionType, mybir.AxisListType.X

    x_blocks = x_in.rearrange("b (n p) d -> b p n d", p=P)
    out_blocks = out.rearrange("b (n p) d -> b p n d", p=P)
    parts_dram = [nc.dram_tensor(f"parts{n}_dram", (2, PARTS, P, 2, T), bf16, kind="Internal").ap() for n in range(2)]
    rsum_dram = nc.dram_tensor("rsum_dram", (QH, T), f32, kind="Internal").ap()

    with ExitStack() as ctx:
        def sb(name, shape, dt=f32):
            return ctx.enter_context(nc.sbuf_tensor(name, shape, dt))

        def sem(name):
            return ctx.enter_context(nc.semaphore(name))

        wqk = sb("wqk", [P, KD, 4, P])
        bqk = sb("bqk", [P, 4])
        wv = sb("wv", [P, KD, D + NML])
        bv = sb("bv", [P, D + NML])
        base = sb("base", [P, KD, D])
        wout = sb("wout", [P, KD, D])
        lora = sb("lora", [P, 2, D])
        bo = sb("bo", [P, D])
        bb = sb("bb", [P, D])
        cos = sb("cos", [P, T])
        sin = sb("sin", [P, T])
        identf = sb("identf", [P, P])
        identb = sb("identb", [P, P], bf16)
        maskb = sb("maskb", [P, P], bf16)
        minus_half = sb("minus_half", [P, BLK])
        x = [sb(f"x{n}", [P, BLK, D]) for n in range(2)]
        xn = [sb(f"xn{n}", [P, 2, D]) for n in range(2)]
        xnT = sb("xnT", [P, KD, T])
        bst = sb("bst", [P, BLK, 6])
        mv = sb("mv", [P, BLK, 2])
        veps = sb("veps", [P, BLK])
        rstd = sb("rstd", [P, BLK])
        rot = sb("rot", [P, 4, HALF])
        parts = sb("parts", [P, PARTS, 2, HALF], bf16)
        qs = [sb(f"qs{g}", [MROWS, QH, T], bf16) for g in range(QUADS)]
        ks = [sb(f"ks{g}", [MROWS, QH, T], bf16) for g in range(QUADS)]
        v_aug = [sb(f"v_aug{n}", [P, BLK, H, VC]) for n in range(2)]
        ml = sb("ml", [P, BLK, NML])
        gmax = sb("gmax", [P, BLK])
        glog = sb("glog", [P, BLK, E])
        gexp = sb("gexp", [P, BLK, E])
        gsum = sb("gsum", [P, BLK])
        gate = sb("gate", [P, BLK, E], bf16)
        gm = sb("gm", [P, BLK, E, R])
        gmT = sb("gmT", [P, BLK // 2, P])
        pmax = sb("pmax", [P, QH, BLK, 2])
        rmax = sb("rmax", [P, QH, BLK])
        mres = sb("mres", [QH * BLK, P])
        mrow = sb("mrow", [QH * BLK, PARTS, P], bf16)
        pt = [sb(f"pt{n}", [P, T]) for n in range(PT_RING)]
        oev = sb("oev", [P, 2, HALF])
        su = sb("su", [QH * BLK, P])
        su_inv = sb("su_inv", [QH * BLK, P])
        oc = sb("oc", [P, 2, T])
        sc = sb("sc", [P, T])

        exp_ps = [ctx.enter_context(nc.psum_tensor(f"exp_ps{n}", [P, T], f32)) for n in range(EXP_RING)]
        max_ps = [ctx.enter_context(nc.psum_tensor(f"max_ps{n}", [P, HALF], f32)) for n in range(2)]
        pv_ps = ctx.enter_context(nc.psum_tensor("pv_ps", [P, HALF], f32))
        misc = ctx.enter_context(nc.psum_tensor("misc", [P, HALF], f32))

        weights_landed = sem("weights_landed")
        ident_ready = sem("ident_ready")
        consts_ready = sem("consts_ready")
        bias_ready = sem("bias_ready")
        pool_steps = sem("pool_steps")
        x_landed = [sem(f"x_landed{n}") for n in range(2)]
        mv_ready = sem("mv_ready")
        stat_steps = sem("stat_steps")
        rstd_steps = sem("rstd_steps")
        xn_ready = sem("xn_ready")
        xb_ready = sem("xb_ready")
        misc_filled = sem("misc_filled")
        misc_drained = sem("misc_drained")
        rot_in = sem("rot_in")
        rot_steps = sem("rot_steps")
        cast_steps = sem("cast_steps")
        parts_landed = sem("parts_landed")
        stack_landed = [sem(f"stack_landed{g}") for g in range(QUADS)]
        rows_landed = [sem(f"rows_landed{g}") for g in range(QUADS)]
        v_ready = sem("v_ready")
        gate_steps = sem("gate_steps")
        gate_exp = sem("gate_exp")
        max_scored = sem("max_scored")
        max_reduced = sem("max_reduced")
        quad_steps = sem("quad_steps")
        rmax_ready = sem("rmax_ready")
        mrow_ready = sem("mrow_ready")
        scored = sem("scored")
        exped = sem("exped")
        masked = sem("masked")
        pv_done = sem("pv_done")
        evacuated = sem("evacuated")
        halves_landed = [sem(f"halves_landed{n}") for n in range(2)]
        recip_ready = sem("recip_ready")
        rsum_landed = sem("rsum_landed")
        sc_landed = sem("sc_landed")
        attn_ready = sem("attn_ready")
        stored = sem("stored")

        block = ctx.enter_context(nc.Block())

        DIAG = len(MASK_REGIONS)

        def misc_count(b, kind, idx):
            if b is None:
                return FIRST_ORDER.index((kind, idx))
            order = LAST_ORDER if isinstance(b, int) and b == B - 1 else BANK_ORDER
            return NFIRST - 4 + NBANK * b + order.index((kind, idx))

        def misc_of(bb_, kind, idx):
            return misc_count(None, kind, idx) if isinstance(bb_, int) and bb_ == 0 else misc_count(bb_ - 1, kind, idx)

        def is_zero(v):
            return isinstance(v, int) and v == 0

        def wait_alone(eng, semaphore, count):
            if not isinstance(count, int):
                count = eng.to_reg(count)
            eng.wait_ge(ident_ready, 1)
            eng.wait_ge(semaphore, count)

        def run_periods(eng, first, period, end):
            first()
            period(0, 0)
            with eng.Fori(0, (B - 2) // 2) as i:
                period(i * 2 + 1, 1)
                period(i * 2 + 2, 0)
            period(B - 1, 1)
            end()

        def tasks_at(b, s):
            for slot, kind, idx in TASKS:
                if slot == s:
                    if kind == "O" and is_zero(b):
                        continue
                    if kind not in ("O", "stack3") and isinstance(b, int) and b == B - 1:
                        continue
                    yield kind, idx

        def has_max(b, s):
            return not (isinstance(b, int) and b == B - 1 and s // NREG == QUADS - 1)

        @block.sync
        def _(sp):
            def load_x(bn, par):
                if not is_zero(bn) and not (isinstance(bn, int) and bn == 1):
                    wait_alone(sp, stored, 64 * (bn - 1))
                sp.dma_start(x[par][:], x_blocks[bn]).then_inc(x_landed[par], 16)

            def store(n, bp, par, c):
                wait_alone(sp, misc_drained, n + 1)
                sp.dma_start(out_blocks[bp][:, 2 * c:2 * c + 2, :], x[par][:, 2 * c:2 * c + 2, :]).then_inc(stored, 16)

            def write_parts(bn, par, u):
                qk, half = u // 2, u % 2
                wait_alone(sp, rot_steps, bn * 16 + u * 4 + 4)
                dst = parts_dram[par][qk].rearrange("p q e t -> q p e t")[:, :, :, half * HALF:(half + 1) * HALF]
                for n in range(PARTS):
                    sp.dma_start(dst[:, n], parts[:, n]).then_inc(parts_landed, 16)

            def load_stack(bn, par, g):
                wait_alone(sp, parts_landed, (bn + 1) * 16 * 4 * PARTS)
                if not is_zero(bn):
                    wait_alone(sp, scored, bn * SLOTS - SLOTS + NREG * (g + 1))
                for st, qk, order in ((qs[g], 0, Q_PART), (ks[g], 1, K_PART)):
                    for c, part in enumerate(order):
                        src = parts_dram[par][qk, part].rearrange("(h d) e t -> h (d e) t", h=H)[g * QH:(g + 1) * QH]
                        sp.dma_start(st[c * DH:(c + 1) * DH, :, :], src.rearrange("h r t -> r h t")).then_inc(stack_landed[g], 16)

            def max_rows(bt, g):
                wait_alone(sp, mrow_ready, bt * QUADS + g + 1)
                for c in range(PARTS):
                    sp.dma_start(qs[g][STACK + c:STACK + c + 1, :, :], mrow[:, c, :]).then_inc(rows_landed[g], 16)

            def half_out(b, g, half):
                hh = g // 2
                if half == 0 and g % 2 == 0:
                    if not (is_zero(b) and hh == 0):
                        if not is_zero(b):
                            wait_alone(sp, misc_filled, misc_count(b, "O", 3) + 1)
                wait_alone(sp, evacuated, b * 8 + g * 2 + half + 1)
                if half == 0 and not (is_zero(b) and g == 0):
                    wait_alone(sp, recip_ready, b * QUADS + g)
                for a in range(QH):
                    row = (g % 2 * QH + a) * DH
                    sp.dma_start(oc[row:row + DH, hh, half * HALF:(half + 1) * HALF], oev[32 * a:32 * a + DH, half, :]).then_inc(halves_landed[half], 16)
                    at = a * BLK + half * (BLK // 2)
                    sp.dma_start(su[at:at + BLK // 2, :], oev[32 * a + DH:32 * a + VC, half, :]).then_inc(halves_landed[half], 16)

            def sums_out(b, g):
                q = b * QUADS + g
                wait_alone(sp, recip_ready, q + 1)
                if not (is_zero(b) and g == 0):
                    wait_alone(sp, sc_landed, q * 64)
                sp.dma_start(rsum_dram.rearrange("a (c t) -> (a c) t", t=P), su_inv[:, :]).then_inc(rsum_landed, 16)
                wait_alone(sp, rsum_landed, (q + 1) * 16)
                if g % 2 == 0 and not (is_zero(b) and g == 0):
                    wait_alone(sp, attn_ready, b * 2 + g // 2)
                for a in range(QH):
                    row = (g % 2 * QH + a) * DH
                    sp.dma_start(sc[row:row + DH, :], rsum_dram[a:a + 1, :].broadcast_to([DH, T])).then_inc(sc_landed, 16)

            def first():
                load_x(0, 0)
                for dst, src in ((wqk, wqk_in), (bqk, bqk_in), (cos, cos_in), (sin, sin_in), (wv, wv_in), (base, base_in),
                                 (wout, wout_in), (lora, lora_in), (bv, bv_in), (bo, bo_in), (bb, bb_in)):
                    sp.dma_start(dst[:], src).then_inc(weights_landed, 16)
                load_x(1, 1)
                for u in range(4):
                    write_parts(0, 0, u)
                for g in range(3):
                    load_stack(0, 0, g)
                max_rows(0, 0)

            def period(b, par):
                for s in range(SLOTS):
                    g, r = divmod(s, NREG)
                    if g == 0 and r == 3 and not is_zero(b):
                        half_out(b - 1, QUADS - 1, 1)
                    if g == 0 and r == 5 and not is_zero(b):
                        sums_out(b - 1, QUADS - 1)
                    if g > 0 and r == 3:
                        half_out(b, g - 1, 1)
                    if g > 0 and r == 5:
                        sums_out(b, g - 1)
                    if r == (15 if g == 0 else 9):
                        half_out(b, g, 0)
                    for kind, idx in tasks_at(b, s):
                        if kind == "stack3":
                            load_stack(b, par, 3)
                        elif kind == "stack":
                            load_stack(b + 1, 1 - par, idx)
                        elif kind == "load_x" and not is_zero(b):
                            load_x(b + 1, 1 - par)
                        elif kind == "O" and idx > 0:
                            store(misc_count(b, "O", idx - 1), b - 1, 1 - par, idx - 1)
                    if s == 15 - 1 and not is_zero(b):
                        store(misc_count(b, "O", 3), b - 1, 1 - par, 3)
                    if s in (29, 34, 39, 44) and not (isinstance(b, int) and b == B - 1):
                        write_parts(b + 1, 1 - par, (s - 29) // 5)
                    if r == MT_SLOT + 1 and has_max(b, s):
                        if g < QUADS - 1:
                            max_rows(b, g + 1)
                        else:
                            max_rows(b + 1, 0)

            def end():
                half_out(B - 1, QUADS - 1, 1)
                sums_out(B - 1, QUADS - 1)
                for c in range(4):
                    store(END_BASE + c, B - 1, 1, c)
                wait_alone(sp, stored, 64 * B)
                wait_alone(sp, rsum_landed, 16 * QUADS * B)
                wait_alone(sp, parts_landed, 16 * 4 * PARTS * B)

            run_periods(sp, first, period, end)

        @block.tensor
        def _(pe):
            def bank_free(n):
                if not is_zero(n):
                    pe.wait_ge(misc_drained, n)

            def transposes(bn, c):
                bank_free(misc_of(bn, "T", c))
                pe.wait_ge(xn_ready, bn * 4 + c + 1)
                for k in range(KD):
                    for m in range(2):
                        last = nc.tensor.transpose(misc[:, k * 256 + m * P:k * 256 + (m + 1) * P], xn[c % 2][:, m, k * P:(k + 1) * P], identf[:])
                last.then_inc(misc_filled, 1)

            def project_qk(bn, u):
                bank_free(misc_of(bn, "QK", u))
                tile_, half = 2 * (u // 4) + u % 2, u // 2 % 2
                for k in range(KD):
                    last = nc.tensor.matmul(misc[:, :], wqk[:, k, tile_, :], xnT[:, k, half * HALF:(half + 1) * HALF], start=(k == 0), stop=(k == KD - 1))
                last.then_inc(misc_filled, 1)

            def project_v(bn, i):
                bank_free(misc_of(bn, "V", i))
                for k in range(KD):
                    last = nc.tensor.matmul(misc[:, 0:D + NML], xnT[:, k, i * P:(i + 1) * P], wv[:, k, :], start=(k == 0), stop=(k == KD - 1))
                last.then_inc(misc_filled, 1)

            def transpose_gates(bn):
                bank_free(misc_of(bn, "GT", 0))
                pe.wait_ge(gate_steps, bn * 6 + 6)
                for c in range(BLK // 2):
                    last = nc.tensor.transpose(misc[:, c * P:(c + 1) * P], gm[:, 2 * c:2 * c + 2, :, :].rearrange("p n e r -> p (n e r)"), identf[:])
                last.then_inc(misc_filled, 1)

            def ffn(bn, c):
                bank_free(misc_of(bn, "F", c))
                for m in range(2):
                    dst, i = misc[:, m * D:(m + 1) * D], 2 * c + m
                    for k in range(KD):
                        nc.tensor.matmul(dst, xnT[:, k, i * P:(i + 1) * P], base[:, k, :], start=(k == 0), stop=False)
                    last = nc.tensor.matmul(dst, gmT[:, c, :], lora[:, m, :], start=False, stop=True)
                last.then_inc(misc_filled, 1)

            def out_product(n, bp, c):
                bank_free(n)
                if c == 0:
                    pe.wait_ge(attn_ready, bp * 2 + 2)
                for m in range(2):
                    i = 2 * c + m
                    for k in range(KD):
                        last = nc.tensor.matmul(misc[:, m * D:(m + 1) * D], oc[:, k, i * P:(i + 1) * P], wout[:, k, :], start=(k == 0), stop=(k == KD - 1))
                last.then_inc(misc_filled, 1)

            def transpose_max(n, q):
                bank_free(n)
                pe.wait_ge(rmax_ready, q + 1)
                nc.tensor.transpose(misc[0:QH * BLK, 0:P], rmax[:].rearrange("p h i -> p (h i)"), identf[:]).then_inc(misc_filled, 1)

            def max_bank(bt, g, m):
                i, _, key0, w, heads = MAX_BANKS[m]
                q = bt * QUADS + g
                if m == 0:
                    pe.wait_ge(stack_landed[g], (bt + 1) * 192)
                if not (is_zero(q) and m < 2):
                    pe.wait_ge(max_reduced, q * NMAX + m - 1)
                bank = max_ps[m % 2]
                diag = key0 + w == (i + 1) * P
                for n, h in enumerate(heads):
                    last = nc.tensor.matmul(bank[:, n * w:(n + 1) * w], qs[g][0:STACK, h, i * P:(i + 1) * P], ks[g][0:STACK, h, key0:key0 + w], start=True, stop=not diag)
                    if diag:
                        last = nc.tensor.matmul(bank[:, (n + 1) * w - P:(n + 1) * w], identb[:], maskb[:], start=False, stop=True)
                last.then_inc(max_scored, 1)

            def score_region(b, g, r):
                n = b * SLOTS + g * NREG + r
                kind, half, j, h0 = REGIONS[r]
                t0 = half * HALF
                if r == 0:
                    pe.wait_ge(rows_landed[g], (b + 1) * 48)
                if not (isinstance(n, int) and n < EXP_RING):
                    pe.wait_ge(exped, n - EXP_RING + 1)
                ps = exp_ps[(g * NREG + r) % EXP_RING]
                if kind == "A":
                    todo = [(a * HALF, h0 + a, j, 0) for a in range(2)]
                elif kind == "B":
                    todo = [(a * HALF + o, h0 + a, jj, f) for a in range(2) for o, jj, f in ((0, j, P), (3 * P, j + 2, 3 * P))]
                else:
                    todo = [(h * 2 * P, h, j, 2 * P) for h in range(QH)]
                for at, h, jj, f in todo:
                    w = HALF - f
                    last = nc.tensor.matmul(ps[:, at:at + w], ks[g][0:MROWS, h, jj * P:(jj + 1) * P], qs[g][0:MROWS, h, t0 + f:t0 + HALF], start=True, stop=True)
                last.then_inc(scored, 1)

            def pv_unit(b, par, g, unit):
                half, kind, j, regions = unit
                q0 = b * SLOTS + g * NREG
                if regions[0] == 0 and g == 0:
                    pe.wait_ge(v_ready, b * BLK + BLK)
                pe.wait_ge(exped, q0 + regions[-1] + 1)
                if j >= 4 * half:
                    pe.wait_ge(masked, (b * QUADS + g) * DIAG + MASK_REGIONS.index(regions[-1]) + 1)
                if j == 0 and not (is_zero(b) and g == 0 and half == 0):
                    pe.wait_ge(evacuated, (b * QUADS + g) * 2 + half)
                for h in range(QH):
                    r = regions[h // 2] if kind != "C" else regions[0]
                    src = pt[(g * NREG + r) % PT_RING]
                    if kind == "A":
                        todo = [(h % 2 * HALF, j, 0)]
                    elif kind == "B":
                        todo = [(h % 2 * HALF, j, P), (h % 2 * HALF + 3 * P, j + 2, 3 * P)]
                    else:
                        todo = [(h * 2 * P, j, 2 * P)]
                    for at, jj, f in todo:
                        last = nc.tensor.matmul(pv_ps[32 * h:32 * h + VC, f:HALF], v_aug[par][:, jj, g * QH + h, :], src[:, at:at + HALF - f],
                                                start=(j == 0), stop=(kind == "C"))
                    if h == QH - 1 or (h == 1 and kind != "C"):
                        last.then_inc(pv_done, 1)

            def late_pv(b, par, s):
                g, r = divmod(s - LAG, NREG)
                for unit in PV_UNITS:
                    if unit[3][-1] == r:
                        pv_unit(b, par, g, unit)

            def first():
                pe.wait_ge(ident_ready, 1)
                pe.wait_ge(weights_landed, 16 * 11)
                for c in range(4):
                    transposes(0, c)
                for u in range(8):
                    project_qk(0, u)
                for i in range(BLK):
                    project_v(0, i)
                transpose_gates(0)
                for c in range(4):
                    ffn(0, c)
                pe.wait_ge(consts_ready, 1)
                for m in range(NMAX):
                    max_bank(0, 0, m)
                transpose_max(misc_count(None, "MT", -1), 0)

            def period(b, par):
                for s in range(SLOTS):
                    g, r = divmod(s, NREG)
                    score_region(b, g, r)
                    if has_max(b, s):
                        for m in range(MAX_PER_SLOT * r, min(MAX_PER_SLOT * (r + 1), NMAX)):
                            if g < QUADS - 1:
                                max_bank(b, g + 1, m)
                            else:
                                max_bank(b + 1, 0, m)
                    if s >= LAG:
                        late_pv(b, par, s)
                    elif not is_zero(b):
                        late_pv(b - 1, 1 - par, s + SLOTS)
                    for kind, idx in tasks_at(b, s):
                        if kind == "O":
                            out_product(misc_count(b, "O", idx), b - 1, idx)
                        elif kind == "T":
                            transposes(b + 1, idx)
                        elif kind == "QK":
                            project_qk(b + 1, idx)
                        elif kind == "V":
                            project_v(b + 1, idx)
                        elif kind == "GT":
                            transpose_gates(b + 1)
                        elif kind == "F":
                            ffn(b + 1, idx)
                    if r == MT_SLOT and has_max(b, s):
                        transpose_max(misc_count(b, "MT", g), b * QUADS + g + 1)

            def end():
                for s in range(LAG):
                    late_pv(B - 1, 1, SLOTS + s)
                for c in range(4):
                    out_product(END_BASE + c, B - 1, c)

            run_periods(pe, first, period, end)

        @block.scalar
        def _(act):
            def drain_misc(dst, n):
                act.wait_ge(misc_filled, n + 1)
                nc.scalar.activation(dst, misc[:, :] if len(dst.shape) == 2 else misc[:, :].rearrange("p (a n) -> p a n", a=dst.shape[1]), ACT.Copy).then_inc(misc_drained, 1)

            def transposed_rows(bn, c):
                drain_misc(xnT[:, :, c * 256:(c + 1) * 256], misc_of(bn, "T", c))

            def transposed_gates(bn):
                drain_misc(gmT[:, :, :], misc_of(bn, "GT", 0))

            def part(bn, u, n):
                if n == 0 and not (is_zero(bn) and u == 0):
                    act.wait_ge(parts_landed, (bn * 4 + u) * 16 * PARTS)
                act.wait_ge(rot_steps, bn * 16 + u * 4 + (2 if n == 0 else 3))
                nc.scalar.activation(parts[:, n, :, :], rot[:, 2 * n:2 * n + 2, :], ACT.Copy).then_inc(cast_steps, 1)

            def gate_exps(bn):
                act.wait_ge(gate_steps, bn * 6 + 2)
                nc.scalar.activation(gexp[:], glog[:], ACT.Exp).then_inc(gate_exp, 1)

            def exp_region(b, g, r):
                n = b * SLOTS + g * NREG + r
                act.wait_ge(scored, n + 1)
                if not (isinstance(n, int) and n < PT_RING):
                    act.wait_ge(pv_done, n - PT_RING + 1)
                nc.scalar.activation(pt[(g * NREG + r) % PT_RING][:], exp_ps[(g * NREG + r) % EXP_RING][:], ACT.Exp, scale=SCORE_SCALE).then_inc(exped, 1)

            def evacuate(b, g, half):
                act.wait_ge(pv_done, b * SLOTS + g * NREG + HALF_END[half] + 1)
                if not (is_zero(b) and g == 0):
                    act.wait_ge(halves_landed[half], (b * QUADS + g) * 128)
                nc.scalar.activation(oev[:, half, :], pv_ps[:, :], ACT.Copy).then_inc(evacuated, 1)

            def first():
                for c in range(4):
                    transposed_rows(0, c)
                for u in range(4):
                    part(0, u, 0)
                    part(0, u, 1)
                gate_exps(0)
                transposed_gates(0)

            def period(b, par):
                for s in range(SLOTS):
                    g, r = divmod(s, NREG)
                    exp_region(b, g, r)
                    if r == LAG + HALF_END[0]:
                        evacuate(b, g, 0)
                    if r == LAG - 1:
                        if g > 0:
                            evacuate(b, g - 1, 1)
                        elif not is_zero(b):
                            evacuate(b - 1, QUADS - 1, 1)
                    for kind, idx in tasks_at(b, s):
                        if kind == "T":
                            transposed_rows(b + 1, idx)
                        elif kind == "GT":
                            transposed_gates(b + 1)
                    if not (isinstance(b, int) and b == B - 1):
                        for u in range(4):
                            if s == 26 + 5 * u:
                                part(b + 1, u, 0)
                            if s == 28 + 5 * u:
                                part(b + 1, u, 1)
                        if s == 45:
                            gate_exps(b + 1)

            def end():
                evacuate(B - 1, QUADS - 1, 1)

            run_periods(act, first, period, end)

        @block.vector
        def _(dve):
            def statistics(bn, par):
                dve.wait_ge(x_landed[par], bn * 8 + (8 if par else 16))
                for i in range(BLK):
                    last = nc.vector.bn_stats(bst[:, i, :], x[par][:, i, :])
                last.then_inc(stat_steps, 1)
                wait_alone(dve, stat_steps, bn + 1)
                for i in range(BLK):
                    last = nc.vector.bn_aggr(mv[:, i, :], bst[:, i, :])
                last.then_inc(mv_ready, 1)

            def normalise(bn, par, c):
                dve.wait_ge(mv_ready, bn + 1)
                dve.wait_ge(rstd_steps, bn * 2 + 2)
                if not (is_zero(bn) and c < 2):
                    n = misc_of(bn, "T", c - 2) if c >= 2 else misc_of(bn - 1, "T", c + 2)
                    dve.wait_ge(misc_filled, n + 1)
                for m in range(2):
                    i = 2 * c + m
                    last = nc.vector.tensor_scalar(xn[c % 2][:, m, :], x[par][:, i, :], mv[:, i, 0:1], rstd[:, i:i + 1], ALU.subtract, ALU.mult)
                last.then_inc(xn_ready, 1)

            def rotate(bn, u):
                unit, eo, half, tile_ = u // 2, u % 2, u // 2 % 2, 2 * (u // 4) + u % 2
                dve.wait_ge(misc_filled, misc_of(bn, "QK", u) + 1)
                if eo == 0 and not (is_zero(bn) and unit == 0):
                    dve.wait_ge(rot_steps, bn * 16 + unit * 4)
                cols = slice(half * HALF, (half + 1) * HALF)
                for dst, table, at_end in ((0 + eo, (cos, sin)[eo], False), (2 + eo, (sin, cos)[eo], True)):
                    last = nc.vector.scalar_tensor_tensor(rot[:, dst, :], misc[:, :], bqk[:, tile_:tile_ + 1], table[:, cols], ALU.add, ALU.mult)
                    if not at_end:
                        last.then_inc(rot_in, 1)
                last.then_inc(misc_drained, 1)

            def values(bn, par, i):
                dve.wait_ge(misc_filled, misc_of(bn, "V", i) + 1)
                if i == 0 and not is_zero(bn) and not (isinstance(bn, int) and bn == 1):
                    dve.wait_ge(pv_done, bn * SLOTS - SLOTS)
                nc.vector.tensor_tensor(v_aug[par][:, i, :, 0:DH], misc[:, 0:D].rearrange("p (h d) -> p h d", d=DH),
                                        bv[:, 0:D].rearrange("p (h d) -> p h d", d=DH), ALU.add).then_inc(v_ready, 1)
                nc.vector.tensor_tensor(ml[:, i, :], misc[:, D:D + NML], bv[:, D:D + NML], ALU.add).then_inc(misc_drained, 1)

            def gate_logits(bn):
                dve.wait_ge(misc_drained, misc_of(bn, "V", BLK - 1) + 1)
                logits = ml[:, :, R:NML]
                nc.vector.tensor_reduce(gmax[:], logits, AX, ALU.max).then_inc(gate_steps, 1)
                dve.wait_ge(gate_steps, bn * 6 + 1)
                nc.vector.tensor_tensor(glog[:], logits, gmax[:].unsqueeze(2).broadcast_to([P, BLK, E]), ALU.subtract).then_inc(gate_steps, 1)

            def gates(bn):
                dve.wait_ge(gate_exp, bn + 1)
                nc.vector.tensor_reduce(gsum[:], gexp[:], AX, ALU.add).then_inc(gate_steps, 1)
                dve.wait_ge(gate_steps, bn * 6 + 3)
                nc.vector.reciprocal(gmax[:], gsum[:]).then_inc(gate_steps, 1)
                dve.wait_ge(gate_steps, bn * 6 + 4)
                nc.vector.tensor_tensor(gate[:], gexp[:], gmax[:].unsqueeze(2).broadcast_to([P, BLK, E]), ALU.mult).then_inc(gate_steps, 1)
                dve.wait_ge(gate_steps, bn * 6 + 5)
                for i in range(BLK):
                    last = nc.vector.scalar_tensor_tensor(gm[:, i], gate[:, i].unsqueeze(2).broadcast_to([P, E, R]), SCALING,
                                                          ml[:, i, 0:R].unsqueeze(1).broadcast_to([P, E, R]), ALU.mult, ALU.mult)
                last.then_inc(gate_steps, 1)

            def add_ffn(bn, par, c):
                dve.wait_ge(misc_filled, misc_of(bn, "F", c) + 1)
                if c == 0:
                    dve.wait_ge(xb_ready, bn + 1)
                rows = x[par][:, 2 * c:2 * c + 2, :]
                nc.vector.tensor_tensor(rows, misc[:, :].rearrange("p (n d) -> p n d", n=2), rows, ALU.add).then_inc(misc_drained, 1)

            def add_attention(n, bp, par, c):
                dve.wait_ge(misc_filled, n + 1)
                rows = x[par][:, 2 * c:2 * c + 2, :]
                nc.vector.tensor_tensor(rows, misc[:, :].rearrange("p (n d) -> p n d", n=2), rows, ALU.add).then_inc(misc_drained, 1)

            def reduce_bank(bt, g, m):
                i, c, _, w, heads = MAX_BANKS[m]
                q = bt * QUADS + g
                dve.wait_ge(max_scored, q * NMAX + m + 1)
                if m == 0 and not is_zero(q):
                    dve.wait_ge(rmax_ready, q)
                nc.vector.tensor_reduce(pmax[:, heads[0]:heads[-1] + 1, i, c], max_ps[m % 2][:, 0:len(heads) * w].rearrange("p (h w) -> p h w", w=w),
                                        AX, ALU.max).then_inc(max_reduced, 1)

            def row_max(bt, g):
                q = bt * QUADS + g
                dve.wait_ge(max_reduced, (q + 1) * NMAX)
                nc.vector.tensor_tensor(rmax[:], pmax[:, :, :, 0], pmax[:, :, :, 1], ALU.max).then_inc(rmax_ready, 1)

            def max_parts(n, bt, g):
                q = bt * QUADS + g
                dve.wait_ge(misc_filled, n + 1)
                if not is_zero(q):
                    dve.wait_ge(rows_landed[(g - 1) % QUADS], (bt + 1) * 48 if g > 0 else bt * 48)
                neg = misc[0:QH * BLK, 0:P]
                nc.vector.tensor_scalar(mrow[:, 0, :], neg, -1.0, None, ALU.mult).then_inc(quad_steps, 1)
                dve.wait_ge(quad_steps, q * 2 + 1)
                nc.vector.scalar_tensor_tensor(mres[:], neg, -1.0, mrow[:, 0, :], ALU.mult, ALU.subtract).then_inc(misc_drained, 1)
                dve.wait_ge(misc_drained, n + 1)
                nc.vector.tensor_copy(mrow[:, 1, :], mres[:]).then_inc(quad_steps, 1)
                dve.wait_ge(quad_steps, q * 2 + 2)
                nc.vector.tensor_tensor(mrow[:, 2, :], mres[:], mrow[:, 1, :], ALU.subtract).then_inc(mrow_ready, 1)

            def invert_sums(b, g):
                q = b * QUADS + g
                for half in range(2):
                    dve.wait_ge(halves_landed[half], (q + 1) * 128)
                if not (is_zero(b) and g == 0):
                    dve.wait_ge(rsum_landed, q * 16)
                nc.vector.reciprocal(su_inv[:], su[:]).then_inc(recip_ready, 1)

            def first():
                nc.vector.memset(pv_ps[:], 0.0)
                nc.vector.memset(pmax[:], -3e38)
                for n in range(2):
                    nc.vector.memset(v_aug[n][:, :, :, DH:VC], 1.0)
                for g in range(QUADS):
                    last = nc.vector.memset(ks[g][STACK:MROWS, :, :], 1.0)
                last.then_inc(consts_ready, 1)
                statistics(0, 0)
                dve.wait_ge(weights_landed, 16 * 11)
                for c in range(4):
                    normalise(0, 0, c)
                for u in range(8):
                    rotate(0, u)
                for i in range(BLK):
                    values(0, 0, i)
                gate_logits(0)
                gates(0)
                for c in range(4):
                    add_ffn(0, 0, c)
                for m in range(NMAX):
                    reduce_bank(0, 0, m)
                row_max(0, 0)
                max_parts(misc_count(None, "MT", -1), 0, 0)

            def period(b, par):
                for s in range(SLOTS):
                    g, r = divmod(s, NREG)
                    if has_max(b, s):
                        bt, gt = (b, g + 1) if g < QUADS - 1 else (b + 1, 0)
                        for m in range(MAX_PER_SLOT * r, min(MAX_PER_SLOT * (r + 1), NMAX)):
                            reduce_bank(bt, gt, m)
                            if m == NMAX - 1:
                                row_max(bt, gt)
                    if r == 5:
                        if g > 0:
                            invert_sums(b, g - 1)
                        elif not is_zero(b):
                            invert_sums(b - 1, QUADS - 1)
                    for kind, idx in tasks_at(b, s):
                        if kind == "O":
                            add_attention(misc_count(b, "O", idx), b - 1, 1 - par, idx)
                        elif kind == "stats":
                            statistics(b + 1, 1 - par)
                        elif kind == "T":
                            normalise(b + 1, 1 - par, idx)
                        elif kind == "QK":
                            rotate(b + 1, idx)
                        elif kind == "V":
                            values(b + 1, 1 - par, idx)
                        elif kind == "gate":
                            gate_logits(b + 1)
                        elif kind == "F":
                            add_ffn(b + 1, 1 - par, idx)
                    if s == 47 and not (isinstance(b, int) and b == B - 1):
                        gates(b + 1)
                    if r == MT_SLOT and has_max(b, s):
                        max_parts(misc_count(b, "MT", g), bt, gt)

            def end():
                invert_sums(B - 1, QUADS - 1)
                for c in range(4):
                    add_attention(END_BASE + c, B - 1, 1, c)

            run_periods(dve, first, period, end)

        @block.gpsimd
        def _(pool):
            def inverse_deviation(bn):
                wait_alone(pool, mv_ready, bn + 1)
                nc.gpsimd.tensor_scalar(veps[:], mv[:, :, 1], EPS, None, ALU.add).then_inc(rstd_steps, 1)
                pool.wait_ge(rstd_steps, bn * 2 + 1)
                nc.gpsimd.tensor_tensor(rstd[:], veps[:], minus_half[:], ALU.pow).then_inc(rstd_steps, 1)

            def add_biases(bn, par):
                pool.wait_ge(xn_ready, bn * 4 + 4)
                for i in range(BLK):
                    last = nc.gpsimd.tensor_tensor(x[par][:, i, :], x[par][:, i, :], bo[:], ALU.add)
                last.then_inc(xb_ready, 1)

            def rotated(bn, u):
                pool.wait_ge(rot_in, bn * 8 + u * 2 + 2)
                pool.wait_ge(misc_drained, misc_of(bn, "QK", 2 * u + 1) + 1)
                nc.gpsimd.tensor_tensor(rot[:, 0, :], rot[:, 0, :], rot[:, 1, :], ALU.subtract).then_inc(rot_steps, 1)
                pool.wait_ge(rot_steps, bn * 16 + u * 4 + 1)
                nc.gpsimd.tensor_tensor(rot[:, 1, :], rot[:, 2, :], rot[:, 3, :], ALU.add).then_inc(rot_steps, 1)
                pool.wait_ge(rot_steps, bn * 16 + u * 4 + 2)

            def left_over(bn, u, n):
                pool.wait_ge(cast_steps, bn * 8 + u * 2 + n + 1)
                for e in range(2):
                    dst = rot[:, 2 + e, :] if n == 0 else parts[:, 2, e, :]
                    last = nc.gpsimd.tensor_tensor(dst, rot[:, 2 * n + e, :], parts[:, n, e, :], ALU.subtract)
                last.then_inc(rot_steps, 1)

            def mask_region(b, g, r):
                kind = REGIONS[r][0]
                wait_alone(pool, exped, b * SLOTS + g * NREG + r + 1)
                tile_ = pt[(g * NREG + r) % PT_RING]
                n = QH if kind == "C" else 2
                heads = tile_[:, :].rearrange("p (h w) -> p h w", h=n)
                for at in (0, 3 * P) if kind == "B" else (0,):
                    blocks = heads[:, :, at:at + P]
                    last = nc.gpsimd.affine_select(out=blocks, in_=blocks, compare_op=ALU.is_ge, fill=0.0, base=0, pattern=[[0, n], [1, P]],
                                                   channel_multiplier=-1)
                last.then_inc(masked, 1)

            def scale_heads(b, hh):
                pool.wait_ge(sc_landed, (b * QUADS + 2 * hh + 2) * 64)
                for n in range(2):
                    for half in range(2):
                        pool.wait_ge(halves_landed[half], (b * QUADS + 2 * hh + 2) * 128)
                    cols = slice(n * HALF, (n + 1) * HALF)
                    last = nc.gpsimd.tensor_tensor(oc[:, hh, cols], oc[:, hh, cols], sc[:, cols], ALU.mult)
                last.then_inc(attn_ready, 1)

            def first():
                nc.gpsimd.memset(minus_half[:], -0.5)
                nc.gpsimd.memset(identf[:], 0.0)
                nc.gpsimd.memset(identb[:], 0.0)
                nc.gpsimd.memset(maskb[:], 0.0).then_inc(pool_steps, 1)
                pool.wait_ge(pool_steps, 1)
                for m in (identf, identb):
                    nc.gpsimd.affine_select(out=m[:], in_=m[:], compare_op=ALU.not_equal, fill=1.0, base=0, pattern=[[-1, P]], channel_multiplier=1)
                nc.gpsimd.affine_select(out=maskb[:], in_=maskb[:], compare_op=ALU.is_ge, fill=MASKED, base=0, pattern=[[-1, P]],
                                        channel_multiplier=1).then_inc(ident_ready, 1)
                pool.wait_ge(weights_landed, 16 * 11)
                nc.gpsimd.tensor_tensor(bo[:], bo[:], bb[:], ALU.add).then_inc(bias_ready, 1)
                pool.wait_ge(bias_ready, 1)
                inverse_deviation(0)
                add_biases(0, 0)
                for u in range(4):
                    rotated(0, u)
                    left_over(0, u, 0)
                    left_over(0, u, 1)

            def period(b, par):
                last_b = isinstance(b, int) and b == B - 1
                for s in range(SLOTS):
                    g, r = divmod(s, NREG)
                    if r in MASK_REGIONS:
                        mask_region(b, g, r)
                    if r == 8 and g == 2:
                        scale_heads(b, 0)
                    if r == 8 and g == 0 and not is_zero(b):
                        scale_heads(b - 1, 1)
                    if not last_b:
                        if s == 18:
                            inverse_deviation(b + 1)
                        if s == 50:
                            add_biases(b + 1, 1 - par)
                        for u in range(4):
                            if s == 25 + 5 * u:
                                rotated(b + 1, u)
                            if s == 26 + 5 * u:
                                left_over(b + 1, u, 0)
                            if s == 28 + 5 * u:
                                left_over(b + 1, u, 1)

            def end():
                scale_heads(B - 1, 1)

            run_periods(pool, first, period, end)


_INS = ["x_in", "wqk_in", "bqk_in", "wv_in", "bv_in", "base_in", "wout_in", "lora_in", "bo_in", "bb_in", "cos_in", "sin_in"]


def kernel(**inputs):
    import numpy as np
    import concourse.bacc as bacc
    from concourse.bass_utils import run_bass_kernel_spmd

    def rows_of(a):
        return a.reshape(KD, P, -1).transpose(1, 0, 2)

    w = np.asarray(inputs["L0_attn_w_qkv"])
    b = np.asarray(inputs["L0_attn_b_qkv"])
    w_pairs = w[:2 * D].reshape(2, H, DH // 2, 2, D).transpose(0, 3, 1, 2, 4).reshape(4, P, D)
    b_pairs = b[:2 * D].reshape(2, H, DH // 2, 2).transpose(0, 3, 1, 2).reshape(4, P)
    inv_freq = (1.0 / np.float32(10000.0) ** (np.arange(0, DH, 2, dtype=np.float32) / np.float32(DH))).astype(np.float32)
    angle = np.tile(inv_freq, H)[:, None] * np.arange(T, dtype=np.float32)[None, :]
    wv = np.concatenate([w[2 * D:].T, np.asarray(inputs["L0_ffn_lora_A"]), np.asarray(inputs["L0_ffn_router_w"]).T], axis=1)
    bv = np.concatenate([b[2 * D:], np.zeros(R, np.float32), np.asarray(inputs["L0_ffn_router_b"])])
    lora_b = np.asarray(inputs["L0_ffn_lora_B"]).reshape(E * R, D)
    arrays = {
        "x_in": np.asarray(inputs["L0_attn_x"]),
        "wqk_in": w_pairs.reshape(4, P, KD, P).transpose(3, 2, 0, 1),
        "bqk_in": b_pairs.T,
        "wv_in": rows_of(wv),
        "bv_in": np.broadcast_to(bv, (P, D + NML)),
        "base_in": rows_of(np.asarray(inputs["L0_ffn_base_w"]).T),
        "wout_in": rows_of(np.asarray(inputs["L0_attn_w_out"]).T),
        "lora_in": np.stack([np.concatenate([lora_b, np.zeros_like(lora_b)]), np.concatenate([np.zeros_like(lora_b), lora_b])], axis=1),
        "bo_in": np.broadcast_to(np.asarray(inputs["L0_attn_b_out"]), (P, D)),
        "bb_in": np.broadcast_to(np.asarray(inputs["L0_ffn_base_b"]), (P, D)),
        "cos_in": np.cos(angle).astype(np.float32),
        "sin_in": np.sin(angle).astype(np.float32),
    }
    nc = bacc.Bacc("TRN2", target_bir_lowering=False, num_devices=1)
    given, args = {}, []
    for name in _INS:
        a = np.ascontiguousarray(arrays[name])
        given[f"{name}_dram"] = a
        args.append(nc.dram_tensor(f"{name}_dram", a.shape, mybir.dt.from_np(a.dtype), kind="ExternalInput").ap())
    args.append(nc.dram_tensor("out_dram", (B, T, D), mybir.dt.float32, kind="ExternalOutput").ap())
    attention_ffn_block(nc, *args)
    r = run_bass_kernel_spmd(nc, [given], core_ids=[0])
    return r.results[0]["out_dram"]
```

```python
from contextlib import ExitStack

import concourse.bass as bass
from concourse import mybir

B, T, D, H, DH = 16, 1024, 256, 16, 16
E, R = 8, 8
SCALING = 2.0
EPS = 1e-5
SCORE_SCALE = DH ** -0.5
P = 128
BLK = T // P
KD = D // P
HALF = T // 2
QH = 4
QUADS = H // QH
VC = DH + 1
NML = R + E
PARTS = 3
STACK = 6 * DH
MROWS = STACK + PARTS
Q_PART = (0, 0, 1, 0, 1, 2)
K_PART = (0, 1, 0, 2, 1, 0)
MASKED = -1e30

REGIONS = []
PV_UNITS = []
for _half in range(2):
    for _kind, _j in [("A", j) for j in range(4 * _half + 1)] + [("B", 4 * _half + 1), ("C", 4 * _half + 2)]:
        _n = 1 if _kind == "C" else 2
        PV_UNITS.append((_half, _kind, _j, list(range(len(REGIONS), len(REGIONS) + _n))))
        REGIONS += [(_kind, _half, _j, 2 * a) for a in range(_n)]
NREG = len(REGIONS)
SLOTS = NREG * QUADS
MASK_REGIONS = [r for r, (kind, half, j, _) in enumerate(REGIONS) if j >= 4 * half]
HALF_END = [max(u[3][-1] for u in PV_UNITS if u[0] == h) for h in range(2)]
EXP_RING, PT_RING, LAG = 2, 6, 3

MAX_BANKS = []
for _i in range(BLK):
    _c0 = min(_i + 1, 4) * P
    _n = min(QH, HALF // _c0)
    MAX_BANKS += [(_i, 0, 0, _c0, list(range(a, a + _n))) for a in range(0, QH, _n)]
    if _i >= 4:
        _c1 = (_i - 3) * P
        _n = min(QH, HALF // _c1)
        MAX_BANKS += [(_i, 1, HALF, _c1, list(range(a, a + _n))) for a in range(0, QH, _n)]
NMAX = len(MAX_BANKS)
MT_SLOT = 13
assert NMAX % 2 == 0 and SLOTS % PT_RING == 0

UNIT = ((18, 21), (27, 28), (34, 35), (41, 42))
T_AT = (5, 8, 10, 12)
TASKS = sorted(
    [(2, "stack3", 3)]
    + [(s, "load_ln", c) for c, s in enumerate((0, 0, 5, 8))] + [(s, "stats", c) for c, s in enumerate((2, 4, 7, 9))]
    + [(s, "norm", c) for c, s in enumerate((4, 7, 9, 11))] + [(s, "T", c) for c, s in enumerate(T_AT)]
    + [(14 + c, "O", c) for c in range(4)] + [(15 + c, "store", c) for c in range(4)] + [(20, "load_x", 0)]
    + [(UNIT[u // 2][u % 2], "QK", u) for u in range(8)]
    + [(e, "rotated", u) for u, (_, e) in enumerate(UNIT)] + [(e + 2, "part0", u) for u, (_, e) in enumerate(UNIT)]
    + [(e + 2, "left0", u) for u, (_, e) in enumerate(UNIT)] + [(e + 4, "part1", u) for u, (_, e) in enumerate(UNIT)]
    + [(e + 4, "left1", u) for u, (_, e) in enumerate(UNIT)] + [(e + 5, "write", u) for u, (_, e) in enumerate(UNIT)]
    + [(s, "V", i) for i, s in enumerate((23, 26, 32, 33, 36, 39, 44, 50))]
    + [(48, "stack", 0), (50, "stack", 1), (58, "stack", 2)]
    + [(51, "gate_logits", 0), (52, "gate_exp", 0), (53, "gates", 0), (54, "GT", 0), (49, "bias", 0)]
    + [(s, "F", c) for c, s in enumerate((57, 59, 68, 69))]
)
LOAD = {"O": (0.9, 0.7), "stats": (0.0, 1.0), "norm": (0.0, 0.5), "T": (0.9, 0.0), "QK": (1.8, 1.4), "V": (1.0, 0.6),
        "gates": (0.0, 1.2), "gate_logits": (0.0, 0.3), "GT": (0.9, 0.0), "F": (2.6, 0.7)}
PV_LOAD = {"A": 1.8, "B": 1.9, "C": 1.0}


def spread_max():
    table = []
    for g in range(QUADS):
        load = [[0.5, 0.9 if r == 6 else 0.0] for r in range(NREG)]
        for s, k, _ in TASKS:
            if s // NREG == g:
                for n in range(2):
                    load[s % NREG][n] += LOAD.get(k, (0.0, 0.0))[n]
        for _, k, _, regions in PV_UNITS:
            load[(regions[-1] + LAG) % NREG][0] += PV_LOAD[k]
        count = [0] * MT_SLOT
        for _ in range(NMAX):
            r = min(range(MT_SLOT), key=lambda n: max(load[n][0] + 0.28, load[n][1] + 0.62))
            count[r] += 1
            load[r][0] += 0.28
            load[r][1] += 0.62
        table.append([range(sum(count[:r]), sum(count[:r + 1])) for r in range(MT_SLOT)] + [range(0)] * (NREG - MT_SLOT))
    return table


MAX_AT = spread_max()
BANK_KINDS = ("O", "T", "QK", "V", "GT", "F", "MT")
MTS = [(18 * g + MT_SLOT, "MT", g) for g in range(QUADS)]
BANK_ORDER = [(k, i) for s, k, i in sorted(TASKS + MTS, key=lambda x: (x[0], x[1] == "MT")) if k in BANK_KINDS]
NBANK = len(BANK_ORDER)
PERIOD0_ORDER = [x for x in BANK_ORDER if x[0] != "O"]
LAST_ORDER = [x for x in BANK_ORDER if x[0] == "O" or x in [("MT", g) for g in range(QUADS - 1)]]
FIRST_ORDER = [("T", c) for c in range(4)] + [("QK", u) for u in range(8)] + [("V", i) for i in range(BLK)]
FIRST_ORDER += [("GT", 0)] + [("F", c) for c in range(4)] + [("MT", -1)]
NFIRST = len(FIRST_ORDER)
END_BASE = NFIRST - 4 + NBANK * (B - 1) + len(LAST_ORDER)


def attention_ffn_block(nc, x_in, wqk_in, bqk_in, wv_in, bv_in, base_in, wout_in, lora_in, bo_in, bb_in, cos_in, sin_in, out):
    f32, bf16 = mybir.dt.float32, mybir.dt.bfloat16
    ALU, ACT, AX = mybir.AluOpType, mybir.ActivationFunctionType, mybir.AxisListType.X

    x_blocks = x_in.rearrange("b (n p) d -> b p n d", p=P)
    out_blocks = out.rearrange("b (n p) d -> b p n d", p=P)
    parts_dram = [nc.dram_tensor(f"parts{n}_dram", (2, PARTS, P, 2, T), bf16, kind="Internal").ap() for n in range(2)]
    rsum_dram = nc.dram_tensor("rsum_dram", (QH, T), f32, kind="Internal").ap()

    with ExitStack() as ctx:
        def sb(name, shape, dt=f32):
            return ctx.enter_context(nc.sbuf_tensor(name, shape, dt))

        def sem(name):
            return ctx.enter_context(nc.semaphore(name))

        wqk = sb("wqk", [P, KD, 4, P])
        bqk = sb("bqk", [P, 4])
        wv = sb("wv", [P, KD, D + NML])
        bv = sb("bv", [P, D + NML])
        base = sb("base", [P, KD, D])
        wout = sb("wout", [P, KD, D])
        lora = sb("lora", [P, 2, D])
        bo = sb("bo", [P, D])
        bb = sb("bb", [P, D])
        cos = sb("cos", [P, T])
        sin = sb("sin", [P, T])
        identf = sb("identf", [P, P])
        identb = sb("identb", [P, P], bf16)
        maskb = sb("maskb", [P, P], bf16)
        minus_half = sb("minus_half", [P, BLK])
        x = [sb(f"x{n}", [P, BLK, D]) for n in range(2)]
        x_ln = [sb(f"x_ln{n}", [P, 2, D]) for n in range(2)]
        xn = [sb(f"xn{n}", [P, 2, D]) for n in range(2)]
        staged = [sb(f"staged{n}", [P, 2, D]) for n in range(2)]
        xnT = sb("xnT", [P, KD, T])
        bst = sb("bst", [P, BLK, 6])
        mv = sb("mv", [P, BLK, 2])
        veps = sb("veps", [P, BLK])
        rstd = sb("rstd", [P, BLK])
        rot = sb("rot", [P, 4, HALF])
        parts = sb("parts", [P, PARTS, 2, HALF], bf16)
        qs = [sb(f"qs{g}", [MROWS, QH, T], bf16) for g in range(QUADS)]
        ks = [sb(f"ks{g}", [MROWS, QH, T], bf16) for g in range(QUADS)]
        v_aug = [sb(f"v_aug{n}", [P, BLK, H, VC]) for n in range(2)]
        ml = sb("ml", [P, BLK, NML])
        gmax = sb("gmax", [P, BLK])
        glog = sb("glog", [P, BLK, E])
        gexp = sb("gexp", [P, BLK, E])
        gsum = sb("gsum", [P, BLK])
        gate = sb("gate", [P, BLK, E], bf16)
        gm = sb("gm", [P, BLK, E, R])
        gmT = sb("gmT", [P, BLK // 2, P])
        pmax = sb("pmax", [P, QH, BLK, 2])
        rmax = sb("rmax", [P, QH, BLK])
        mres = sb("mres", [QH * BLK, P])
        mrow = sb("mrow", [QH * BLK, PARTS, P], bf16)
        pt = [sb(f"pt{n}", [P, T]) for n in range(PT_RING)]
        oev = sb("oev", [P, 2, HALF])
        su = sb("su", [QH * BLK, P])
        su_inv = sb("su_inv", [QH * BLK, P])
        oc = sb("oc", [P, 2, T])
        sc = sb("sc", [P, T])

        exp_ps = [ctx.enter_context(nc.psum_tensor(f"exp_ps{n}", [P, T], f32)) for n in range(EXP_RING)]
        max_ps = [ctx.enter_context(nc.psum_tensor(f"max_ps{n}", [P, HALF], f32)) for n in range(2)]
        pv_ps = ctx.enter_context(nc.psum_tensor("pv_ps", [P, HALF], f32))
        misc = ctx.enter_context(nc.psum_tensor("misc", [P, HALF], f32))

        weights_landed = sem("weights_landed")
        ident_ready = sem("ident_ready")
        consts_ready = sem("consts_ready")
        bias_ready = sem("bias_ready")
        pool_steps = sem("pool_steps")
        x_landed = [sem(f"x_landed{n}") for n in range(2)]
        mv_ready = sem("mv_ready")
        stat_steps = sem("stat_steps")
        rstd_steps = sem("rstd_steps")
        xn_ready = sem("xn_ready")
        xb_ready = sem("xb_ready")
        misc_filled = sem("misc_filled")
        misc_drained = sem("misc_drained")
        rot_in = sem("rot_in")
        rot_steps = sem("rot_steps")
        cast_steps = sem("cast_steps")
        parts_landed = sem("parts_landed")
        stack_landed = [sem(f"stack_landed{g}") for g in range(QUADS)]
        rows_landed = [sem(f"rows_landed{g}") for g in range(QUADS)]
        v_ready = sem("v_ready")
        gate_steps = sem("gate_steps")
        gate_exp = sem("gate_exp")
        max_scored = sem("max_scored")
        max_reduced = sem("max_reduced")
        quad_steps = sem("quad_steps")
        rmax_ready = sem("rmax_ready")
        mrow_ready = sem("mrow_ready")
        scored = sem("scored")
        exped = sem("exped")
        masked = sem("masked")
        pv_done = sem("pv_done")
        evacuated = sem("evacuated")
        halves_landed = [sem(f"halves_landed{n}") for n in range(2)]
        recip_ready = sem("recip_ready")
        rsum_landed = sem("rsum_landed")
        sc_landed = sem("sc_landed")
        attn_ready = sem("attn_ready")
        ln_landed = [sem(f"ln_landed{n}") for n in range(2)]
        stored = [sem(f"stored{n}") for n in range(2)]

        block = ctx.enter_context(nc.Block())

        DIAG = len(MASK_REGIONS)

        def misc_count(b, kind, idx):
            if b is None:
                return FIRST_ORDER.index((kind, idx))
            if is_zero(b):
                return NFIRST + PERIOD0_ORDER.index((kind, idx))
            order = LAST_ORDER if isinstance(b, int) and b == B - 1 else BANK_ORDER
            return NFIRST - 4 + NBANK * b + order.index((kind, idx))

        def misc_of(bb_, kind, idx):
            return misc_count(None, kind, idx) if isinstance(bb_, int) and bb_ == 0 else misc_count(bb_ - 1, kind, idx)

        def is_zero(v):
            return isinstance(v, int) and v == 0

        def wait_alone(eng, semaphore, count):
            if not isinstance(count, int):
                count = eng.to_reg(count)
            eng.wait_ge(ident_ready, 1)
            eng.wait_ge(semaphore, count)

        def run_periods(eng, first, period, end):
            first()
            period(0, 0)
            with eng.Fori(0, (B - 2) // 2) as i:
                period(i * 2 + 1, 1)
                period(i * 2 + 2, 0)
            period(B - 1, 1)
            end()

        def tasks_at(b, s):
            for slot, kind, idx in TASKS:
                if slot == s:
                    if kind in ("O", "store") and is_zero(b):
                        continue
                    if kind not in ("O", "store", "stack3") and isinstance(b, int) and b == B - 1:
                        continue
                    yield kind, idx

        def has_max(b, s):
            return not (isinstance(b, int) and b == B - 1 and s // NREG == QUADS - 1)

        def next_quad(b, g):
            return (b, g + 1) if g < QUADS - 1 else (b + 1, 0)

        def max_banks(b, s):
            return MAX_AT[s // NREG][s % NREG] if has_max(b, s) else range(0)

        @block.sync
        def _(sp):
            def load_x(bn, par):
                if not is_zero(bn) and not (isinstance(bn, int) and bn == 1):
                    wait_alone(sp, misc_drained, misc_count(bn - 1, "O", 3) + 1)
                sp.dma_start(x[par][:], x_blocks[bn]).then_inc(x_landed[par], 16)

            def load_ln(bn, c):
                if not (is_zero(bn) and c < 2):
                    wait_alone(sp, xn_ready, bn * 4 + c - 1)
                sp.dma_start(x_ln[c % 2][:], x_blocks[bn][:, 2 * c:2 * c + 2, :]).then_inc(ln_landed[c % 2], 16)

            def store(n, bp, c):
                wait_alone(sp, misc_drained, n + 1)
                sp.dma_start(out_blocks[bp][:, 2 * c:2 * c + 2, :], staged[c % 2][:]).then_inc(stored[c % 2], 16)

            def write_parts(bn, par, u):
                qk, half = u // 2, u % 2
                wait_alone(sp, rot_steps, bn * 16 + u * 4 + 4)
                dst = parts_dram[par][qk].rearrange("p q e t -> q p e t")[:, :, :, half * HALF:(half + 1) * HALF]
                for n in range(PARTS):
                    sp.dma_start(dst[:, n], parts[:, n]).then_inc(parts_landed, 16)

            def load_stack(bn, par, g):
                wait_alone(sp, parts_landed, (bn + 1) * 16 * 4 * PARTS)
                if not is_zero(bn):
                    wait_alone(sp, scored, bn * SLOTS - SLOTS + NREG * (g + 1))
                for st, qk, order in ((qs[g], 0, Q_PART), (ks[g], 1, K_PART)):
                    for c, part in enumerate(order):
                        src = parts_dram[par][qk, part].rearrange("(h d) e t -> h (d e) t", h=H)[g * QH:(g + 1) * QH]
                        sp.dma_start(st[c * DH:(c + 1) * DH, :, :], src.rearrange("h r t -> r h t")).then_inc(stack_landed[g], 16)

            def max_rows(bt, g):
                wait_alone(sp, mrow_ready, bt * QUADS + g + 1)
                for c in range(PARTS):
                    sp.dma_start(qs[g][STACK + c:STACK + c + 1, :, :], mrow[:, c, :]).then_inc(rows_landed[g], 16)

            def half_out(b, g, half):
                hh = g // 2
                if half == 0 and g % 2 == 0:
                    if not (is_zero(b) and hh == 0):
                        if not is_zero(b):
                            wait_alone(sp, misc_filled, misc_count(b, "O", 3) + 1)
                wait_alone(sp, evacuated, b * 8 + g * 2 + half + 1)
                if half == 0 and not (is_zero(b) and g == 0):
                    wait_alone(sp, recip_ready, b * QUADS + g)
                for a in range(QH):
                    row = (g % 2 * QH + a) * DH
                    sp.dma_start(oc[row:row + DH, hh, half * HALF:(half + 1) * HALF], oev[32 * a:32 * a + DH, half, :]).then_inc(halves_landed[half], 16)
                    at = a * BLK + half * (BLK // 2)
                    sp.dma_start(su[at:at + BLK // 2, :], oev[32 * a + DH:32 * a + VC, half, :]).then_inc(halves_landed[half], 16)

            def sums_out(b, g):
                q = b * QUADS + g
                wait_alone(sp, recip_ready, q + 1)
                if not (is_zero(b) and g == 0):
                    wait_alone(sp, sc_landed, q * 64)
                sp.dma_start(rsum_dram.rearrange("a (c t) -> (a c) t", t=P), su_inv[:, :]).then_inc(rsum_landed, 16)
                wait_alone(sp, rsum_landed, (q + 1) * 16)
                if g % 2 == 0 and not (is_zero(b) and g == 0):
                    wait_alone(sp, attn_ready, b * 2 + g // 2)
                for a in range(QH):
                    row = (g % 2 * QH + a) * DH
                    sp.dma_start(sc[row:row + DH, :], rsum_dram[a:a + 1, :].broadcast_to([DH, T])).then_inc(sc_landed, 16)

            def first():
                load_ln(0, 0)
                load_ln(0, 1)
                for dst, src in ((wqk, wqk_in), (bqk, bqk_in), (cos, cos_in), (sin, sin_in), (wv, wv_in), (base, base_in),
                                 (wout, wout_in), (lora, lora_in), (bv, bv_in), (bo, bo_in), (bb, bb_in)):
                    sp.dma_start(dst[:], src).then_inc(weights_landed, 16)
                load_ln(0, 2)
                load_ln(0, 3)
                load_x(0, 0)
                load_x(1, 1)
                for u in range(4):
                    write_parts(0, 0, u)
                for g in range(3):
                    load_stack(0, 0, g)
                max_rows(0, 0)

            def period(b, par):
                for s in range(SLOTS):
                    g, r = divmod(s, NREG)
                    if g == 0 and r == 3 and not is_zero(b):
                        half_out(b - 1, QUADS - 1, 1)
                    if g == 0 and r == 7 and not is_zero(b):
                        sums_out(b - 1, QUADS - 1)
                    if g > 0 and r == 3:
                        half_out(b, g - 1, 1)
                    if g > 0 and r == 7:
                        sums_out(b, g - 1)
                    if r == 9 and g > 0:
                        half_out(b, g, 0)
                    if g == 1 and r == 1:
                        half_out(b, 0, 0)
                    for kind, idx in tasks_at(b, s):
                        if kind == "stack3":
                            load_stack(b, par, 3)
                        elif kind == "stack":
                            load_stack(b + 1, 1 - par, idx)
                        elif kind == "load_ln":
                            load_ln(b + 1, idx)
                        elif kind == "load_x" and not is_zero(b):
                            load_x(b + 1, 1 - par)
                        elif kind == "store":
                            store(misc_count(b, "O", idx), b - 1, idx)
                        elif kind == "write":
                            write_parts(b + 1, 1 - par, idx)
                    if r == MT_SLOT and has_max(b, s):
                        if g < QUADS - 1:
                            max_rows(b, g + 1)
                        else:
                            max_rows(b + 1, 0)

            def end():
                half_out(B - 1, QUADS - 1, 1)
                sums_out(B - 1, QUADS - 1)
                for c in range(4):
                    store(END_BASE + c, B - 1, c)
                for n in range(2):
                    wait_alone(sp, stored[n], 32 * B)
                wait_alone(sp, rsum_landed, 16 * QUADS * B)
                wait_alone(sp, parts_landed, 16 * 4 * PARTS * B)

            run_periods(sp, first, period, end)

        @block.tensor
        def _(pe):
            def bank_free(n):
                if not is_zero(n):
                    pe.wait_ge(misc_drained, n)

            def transposes(bn, c):
                bank_free(misc_of(bn, "T", c))
                pe.wait_ge(xn_ready, bn * 4 + c + 1)
                for k in range(KD):
                    for m in range(2):
                        last = nc.tensor.transpose(misc[:, k * 256 + m * P:k * 256 + (m + 1) * P], xn[c % 2][:, m, k * P:(k + 1) * P], identf[:])
                last.then_inc(misc_filled, 1)

            def project_qk(bn, u):
                bank_free(misc_of(bn, "QK", u))
                tile_, half = 2 * (u // 4) + u % 2, u // 2 % 2
                for k in range(KD):
                    last = nc.tensor.matmul(misc[:, :], wqk[:, k, tile_, :], xnT[:, k, half * HALF:(half + 1) * HALF], start=(k == 0), stop=(k == KD - 1))
                last.then_inc(misc_filled, 1)

            def project_v(bn, i):
                bank_free(misc_of(bn, "V", i))
                for k in range(KD):
                    last = nc.tensor.matmul(misc[:, 0:D + NML], xnT[:, k, i * P:(i + 1) * P], wv[:, k, :], start=(k == 0), stop=(k == KD - 1))
                last.then_inc(misc_filled, 1)

            def transpose_gates(bn):
                bank_free(misc_of(bn, "GT", 0))
                pe.wait_ge(gate_steps, bn * 6 + 6)
                for c in range(BLK // 2):
                    last = nc.tensor.transpose(misc[:, c * P:(c + 1) * P], gm[:, 2 * c:2 * c + 2, :, :].rearrange("p n e r -> p (n e r)"), identf[:])
                last.then_inc(misc_filled, 1)

            def ffn(bn, c):
                bank_free(misc_of(bn, "F", c))
                for m in range(2):
                    dst, i = misc[:, m * D:(m + 1) * D], 2 * c + m
                    for k in range(KD):
                        nc.tensor.matmul(dst, xnT[:, k, i * P:(i + 1) * P], base[:, k, :], start=(k == 0), stop=False)
                    last = nc.tensor.matmul(dst, gmT[:, c, :], lora[:, m, :], start=False, stop=True)
                last.then_inc(misc_filled, 1)

            def out_product(n, bp, c):
                bank_free(n)
                if c == 0:
                    pe.wait_ge(attn_ready, bp * 2 + 2)
                for m in range(2):
                    i = 2 * c + m
                    for k in range(KD):
                        last = nc.tensor.matmul(misc[:, m * D:(m + 1) * D], oc[:, k, i * P:(i + 1) * P], wout[:, k, :], start=(k == 0), stop=(k == KD - 1))
                last.then_inc(misc_filled, 1)

            def transpose_max(n, q):
                bank_free(n)
                pe.wait_ge(rmax_ready, q + 1)
                nc.tensor.transpose(misc[0:QH * BLK, 0:P], rmax[:].rearrange("p h i -> p (h i)"), identf[:]).then_inc(misc_filled, 1)

            def max_bank(bt, g, m):
                i, _, key0, w, heads = MAX_BANKS[m]
                q = bt * QUADS + g
                if m == 0:
                    pe.wait_ge(stack_landed[g], (bt + 1) * 192)
                if not (is_zero(q) and m < 2):
                    pe.wait_ge(max_reduced, q * NMAX + m - 1)
                bank = max_ps[m % 2]
                diag = key0 + w == (i + 1) * P
                for n, h in enumerate(heads):
                    last = nc.tensor.matmul(bank[:, n * w:(n + 1) * w], qs[g][0:STACK, h, i * P:(i + 1) * P], ks[g][0:STACK, h, key0:key0 + w], start=True, stop=not diag)
                    if diag:
                        last = nc.tensor.matmul(bank[:, (n + 1) * w - P:(n + 1) * w], identb[:], maskb[:], start=False, stop=True)
                last.then_inc(max_scored, 1)

            def score_region(b, g, r):
                n = b * SLOTS + g * NREG + r
                kind, half, j, h0 = REGIONS[r]
                t0 = half * HALF
                if r == 0:
                    pe.wait_ge(rows_landed[g], (b + 1) * 48)
                if not (isinstance(n, int) and n < EXP_RING):
                    pe.wait_ge(exped, n - EXP_RING + 1)
                ps = exp_ps[(g * NREG + r) % EXP_RING]
                if kind == "A":
                    todo = [(a * HALF, h0 + a, j, 0) for a in range(2)]
                elif kind == "B":
                    todo = [(a * HALF + o, h0 + a, jj, f) for a in range(2) for o, jj, f in ((0, j, P), (3 * P, j + 2, 3 * P))]
                else:
                    todo = [(h * 2 * P, h, j, 2 * P) for h in range(QH)]
                for at, h, jj, f in todo:
                    w = HALF - f
                    last = nc.tensor.matmul(ps[:, at:at + w], ks[g][0:MROWS, h, jj * P:(jj + 1) * P], qs[g][0:MROWS, h, t0 + f:t0 + HALF], start=True, stop=True)
                last.then_inc(scored, 1)

            def pv_unit(b, par, g, unit):
                half, kind, j, regions = unit
                q0 = b * SLOTS + g * NREG
                if regions[0] == 0 and g == 0:
                    pe.wait_ge(v_ready, b * BLK + BLK)
                pe.wait_ge(exped, q0 + regions[-1] + 1)
                if j >= 4 * half:
                    pe.wait_ge(masked, (b * QUADS + g) * DIAG + MASK_REGIONS.index(regions[-1]) + 1)
                if j == 0 and not (is_zero(b) and g == 0 and half == 0):
                    pe.wait_ge(evacuated, (b * QUADS + g) * 2 + half)
                for h in range(QH):
                    r = regions[h // 2] if kind != "C" else regions[0]
                    src = pt[(g * NREG + r) % PT_RING]
                    if kind == "A":
                        todo = [(h % 2 * HALF, j, 0)]
                    elif kind == "B":
                        todo = [(h % 2 * HALF, j, P), (h % 2 * HALF + 3 * P, j + 2, 3 * P)]
                    else:
                        todo = [(h * 2 * P, j, 2 * P)]
                    for at, jj, f in todo:
                        last = nc.tensor.matmul(pv_ps[32 * h:32 * h + VC, f:HALF], v_aug[par][:, jj, g * QH + h, :], src[:, at:at + HALF - f],
                                                start=(j == 0), stop=(kind == "C"))
                    if h == QH - 1 or (h == 1 and kind != "C"):
                        last.then_inc(pv_done, 1)

            def late_pv(b, par, s):
                g, r = divmod(s - LAG, NREG)
                for unit in PV_UNITS:
                    if unit[3][-1] == r:
                        pv_unit(b, par, g, unit)

            def first():
                pe.wait_ge(ident_ready, 1)
                pe.wait_ge(weights_landed, 16 * 11)
                for c in range(4):
                    transposes(0, c)
                for u in range(8):
                    project_qk(0, u)
                for i in range(BLK):
                    project_v(0, i)
                transpose_gates(0)
                for c in range(4):
                    ffn(0, c)
                pe.wait_ge(consts_ready, 1)
                for m in range(NMAX):
                    max_bank(0, 0, m)
                transpose_max(misc_count(None, "MT", -1), 0)

            def period(b, par):
                for s in range(SLOTS):
                    g, r = divmod(s, NREG)
                    score_region(b, g, r)
                    banks = max_banks(b, s)
                    for m in banks[0:1]:
                        max_bank(*next_quad(b, g), m)
                    if s >= LAG:
                        late_pv(b, par, s)
                    elif not is_zero(b):
                        late_pv(b - 1, 1 - par, s + SLOTS)
                    for m in banks[1:2]:
                        max_bank(*next_quad(b, g), m)
                    for kind, idx in tasks_at(b, s):
                        if kind == "O":
                            out_product(misc_count(b, "O", idx), b - 1, idx)
                        elif kind == "T":
                            transposes(b + 1, idx)
                        elif kind == "QK":
                            project_qk(b + 1, idx)
                        elif kind == "V":
                            project_v(b + 1, idx)
                        elif kind == "GT":
                            transpose_gates(b + 1)
                        elif kind == "F":
                            ffn(b + 1, idx)
                    for m in banks[2:]:
                        max_bank(*next_quad(b, g), m)
                    if r == MT_SLOT and has_max(b, s):
                        transpose_max(misc_count(b, "MT", g), b * QUADS + g + 1)

            def end():
                for s in range(LAG):
                    late_pv(B - 1, 1, SLOTS + s)
                for c in range(4):
                    out_product(END_BASE + c, B - 1, c)

            run_periods(pe, first, period, end)

        @block.scalar
        def _(act):
            def drain_misc(dst, n):
                act.wait_ge(misc_filled, n + 1)
                nc.scalar.activation(dst, misc[:, :] if len(dst.shape) == 2 else misc[:, :].rearrange("p (a n) -> p a n", a=dst.shape[1]), ACT.Copy).then_inc(misc_drained, 1)

            def transposed_rows(bn, c):
                drain_misc(xnT[:, :, c * 256:(c + 1) * 256], misc_of(bn, "T", c))

            def transposed_gates(bn):
                drain_misc(gmT[:, :, :], misc_of(bn, "GT", 0))

            def part(bn, u, n):
                if n == 0 and not (is_zero(bn) and u == 0):
                    act.wait_ge(parts_landed, (bn * 4 + u) * 16 * PARTS)
                act.wait_ge(rot_steps, bn * 16 + u * 4 + (2 if n == 0 else 3))
                nc.scalar.activation(parts[:, n, :, :], rot[:, 2 * n:2 * n + 2, :], ACT.Copy).then_inc(cast_steps, 1)

            def gate_exps(bn):
                act.wait_ge(gate_steps, bn * 6 + 2)
                nc.scalar.activation(gexp[:], glog[:], ACT.Exp).then_inc(gate_exp, 1)

            def exp_region(b, g, r):
                n = b * SLOTS + g * NREG + r
                act.wait_ge(scored, n + 1)
                if not (isinstance(n, int) and n < PT_RING):
                    act.wait_ge(pv_done, n - PT_RING + 1)
                nc.scalar.activation(pt[(g * NREG + r) % PT_RING][:], exp_ps[(g * NREG + r) % EXP_RING][:], ACT.Exp, scale=SCORE_SCALE).then_inc(exped, 1)

            def evacuate(b, g, half):
                act.wait_ge(pv_done, b * SLOTS + g * NREG + HALF_END[half] + 1)
                if not (is_zero(b) and g == 0):
                    act.wait_ge(halves_landed[half], (b * QUADS + g) * 128)
                nc.scalar.activation(oev[:, half, :], pv_ps[:, :], ACT.Copy).then_inc(evacuated, 1)

            def first():
                for c in range(4):
                    transposed_rows(0, c)
                for u in range(4):
                    part(0, u, 0)
                    part(0, u, 1)
                gate_exps(0)
                transposed_gates(0)

            def period(b, par):
                for s in range(SLOTS):
                    g, r = divmod(s, NREG)
                    exp_region(b, g, r)
                    if r == LAG + HALF_END[0] + 1:
                        evacuate(b, g, 0)
                    if r == LAG:
                        if g > 0:
                            evacuate(b, g - 1, 1)
                        elif not is_zero(b):
                            evacuate(b - 1, QUADS - 1, 1)
                    for kind, idx in tasks_at(b, s):
                        if kind == "T":
                            transposed_rows(b + 1, idx)
                        elif kind == "GT":
                            transposed_gates(b + 1)
                        elif kind == "part0":
                            part(b + 1, idx, 0)
                        elif kind == "part1":
                            part(b + 1, idx, 1)
                        elif kind == "gate_exp":
                            gate_exps(b + 1)

            def end():
                evacuate(B - 1, QUADS - 1, 1)

            run_periods(act, first, period, end)

        @block.vector
        def _(dve):
            def statistics(bn, c):
                dve.wait_ge(ln_landed[c % 2], bn * 32 + (c // 2) * 16 + 16)
                for m in range(2):
                    last = nc.vector.bn_stats(bst[:, 2 * c + m, :], x_ln[c % 2][:, m, :])
                last.then_inc(stat_steps, 1)
                wait_alone(dve, stat_steps, bn * 4 + c + 1)
                for i in (2 * c, 2 * c + 1):
                    last = nc.vector.bn_aggr(mv[:, i, :], bst[:, i, :])
                last.then_inc(mv_ready, 1)

            def normalise(bn, c):
                dve.wait_ge(rstd_steps, bn * 8 + c * 2 + 2)
                if not (is_zero(bn) and c < 2):
                    n = misc_of(bn, "T", c - 2) if c >= 2 else misc_of(bn - 1, "F", 3)
                    dve.wait_ge(misc_filled, n + 1)
                for m in range(2):
                    i = 2 * c + m
                    last = nc.vector.tensor_scalar(xn[c % 2][:, m, :], x_ln[c % 2][:, m, :], mv[:, i, 0:1], rstd[:, i:i + 1], ALU.subtract, ALU.mult)
                last.then_inc(xn_ready, 1)

            def rotate(bn, u):
                unit, eo, half, tile_ = u // 2, u % 2, u // 2 % 2, 2 * (u // 4) + u % 2
                dve.wait_ge(misc_filled, misc_of(bn, "QK", u) + 1)
                if eo == 0 and not (is_zero(bn) and unit == 0):
                    dve.wait_ge(rot_steps, bn * 16 + unit * 4)
                cols = slice(half * HALF, (half + 1) * HALF)
                for dst, table, at_end in ((0 + eo, (cos, sin)[eo], False), (2 + eo, (sin, cos)[eo], True)):
                    last = nc.vector.scalar_tensor_tensor(rot[:, dst, :], misc[:, :], bqk[:, tile_:tile_ + 1], table[:, cols], ALU.add, ALU.mult)
                    if not at_end:
                        last.then_inc(rot_in, 1)
                last.then_inc(misc_drained, 1)

            def values(bn, par, i):
                dve.wait_ge(misc_filled, misc_of(bn, "V", i) + 1)
                if i == 0 and not is_zero(bn) and not (isinstance(bn, int) and bn == 1):
                    dve.wait_ge(pv_done, bn * SLOTS - SLOTS)
                nc.vector.tensor_tensor(v_aug[par][:, i, :, 0:DH], misc[:, 0:D].rearrange("p (h d) -> p h d", d=DH),
                                        bv[:, 0:D].rearrange("p (h d) -> p h d", d=DH), ALU.add).then_inc(v_ready, 1)
                nc.vector.tensor_tensor(ml[:, i, :], misc[:, D:D + NML], bv[:, D:D + NML], ALU.add).then_inc(misc_drained, 1)

            def gate_logits(bn):
                dve.wait_ge(misc_drained, misc_of(bn, "V", BLK - 1) + 1)
                logits = ml[:, :, R:NML]
                nc.vector.tensor_reduce(gmax[:], logits, AX, ALU.max).then_inc(gate_steps, 1)
                dve.wait_ge(gate_steps, bn * 6 + 1)
                nc.vector.tensor_tensor(glog[:], logits, gmax[:].unsqueeze(2).broadcast_to([P, BLK, E]), ALU.subtract).then_inc(gate_steps, 1)

            def gates(bn):
                dve.wait_ge(gate_exp, bn + 1)
                nc.vector.tensor_reduce(gsum[:], gexp[:], AX, ALU.add).then_inc(gate_steps, 1)
                dve.wait_ge(gate_steps, bn * 6 + 3)
                nc.vector.reciprocal(gmax[:], gsum[:]).then_inc(gate_steps, 1)
                dve.wait_ge(gate_steps, bn * 6 + 4)
                nc.vector.tensor_tensor(gate[:], gexp[:], gmax[:].unsqueeze(2).broadcast_to([P, BLK, E]), ALU.mult).then_inc(gate_steps, 1)
                dve.wait_ge(gate_steps, bn * 6 + 5)
                for i in range(BLK):
                    last = nc.vector.scalar_tensor_tensor(gm[:, i], gate[:, i].unsqueeze(2).broadcast_to([P, E, R]), SCALING,
                                                          ml[:, i, 0:R].unsqueeze(1).broadcast_to([P, E, R]), ALU.mult, ALU.mult)
                last.then_inc(gate_steps, 1)

            def add_ffn(bn, par, c):
                dve.wait_ge(misc_filled, misc_of(bn, "F", c) + 1)
                if c == 0:
                    dve.wait_ge(xb_ready, bn + 1)
                rows = x[par][:, 2 * c:2 * c + 2, :]
                nc.vector.tensor_tensor(rows, misc[:, :].rearrange("p (n d) -> p n d", n=2), rows, ALU.add).then_inc(misc_drained, 1)

            def add_attention(n, bp, par, c):
                dve.wait_ge(misc_filled, n + 1)
                if not (is_zero(bp) and c < 2):
                    dve.wait_ge(stored[c % 2], bp * 32 + (c // 2) * 16)
                rows = x[par][:, 2 * c:2 * c + 2, :]
                nc.vector.tensor_tensor(staged[c % 2][:], misc[:, :].rearrange("p (n d) -> p n d", n=2), rows, ALU.add).then_inc(misc_drained, 1)

            def reduce_bank(bt, g, m):
                i, c, _, w, heads = MAX_BANKS[m]
                q = bt * QUADS + g
                dve.wait_ge(max_scored, q * NMAX + m + 1)
                if m == 0 and not is_zero(q):
                    dve.wait_ge(rmax_ready, q)
                nc.vector.tensor_reduce(pmax[:, heads[0]:heads[-1] + 1, i, c], max_ps[m % 2][:, 0:len(heads) * w].rearrange("p (h w) -> p h w", w=w),
                                        AX, ALU.max).then_inc(max_reduced, 1)

            def row_max(bt, g):
                q = bt * QUADS + g
                dve.wait_ge(max_reduced, (q + 1) * NMAX)
                nc.vector.tensor_tensor(rmax[:], pmax[:, :, :, 0], pmax[:, :, :, 1], ALU.max).then_inc(rmax_ready, 1)

            def max_parts(n, bt, g):
                q = bt * QUADS + g
                dve.wait_ge(misc_filled, n + 1)
                if not is_zero(q):
                    dve.wait_ge(rows_landed[(g - 1) % QUADS], (bt + 1) * 48 if g > 0 else bt * 48)
                neg = misc[0:QH * BLK, 0:P]
                nc.vector.tensor_scalar(mrow[:, 0, :], neg, -1.0, None, ALU.mult).then_inc(quad_steps, 1)
                dve.wait_ge(quad_steps, q * 2 + 1)
                nc.vector.scalar_tensor_tensor(mres[:], neg, -1.0, mrow[:, 0, :], ALU.mult, ALU.subtract).then_inc(misc_drained, 1)
                dve.wait_ge(misc_drained, n + 1)
                nc.vector.tensor_copy(mrow[:, 1, :], mres[:]).then_inc(quad_steps, 1)
                dve.wait_ge(quad_steps, q * 2 + 2)
                nc.vector.tensor_tensor(mrow[:, 2, :], mres[:], mrow[:, 1, :], ALU.subtract).then_inc(mrow_ready, 1)

            def invert_sums(b, g):
                q = b * QUADS + g
                for half in range(2):
                    dve.wait_ge(halves_landed[half], (q + 1) * 128)
                if not (is_zero(b) and g == 0):
                    dve.wait_ge(rsum_landed, q * 16)
                nc.vector.reciprocal(su_inv[:], su[:]).then_inc(recip_ready, 1)

            def first():
                nc.vector.memset(pv_ps[:], 0.0)
                nc.vector.memset(pmax[:], -3e38)
                for n in range(2):
                    nc.vector.memset(v_aug[n][:, :, :, DH:VC], 1.0)
                for g in range(QUADS):
                    last = nc.vector.memset(ks[g][STACK:MROWS, :, :], 1.0)
                last.then_inc(consts_ready, 1)
                dve.wait_ge(weights_landed, 16 * 11)
                for c in range(4):
                    statistics(0, c)
                    normalise(0, c)
                for u in range(8):
                    rotate(0, u)
                for i in range(BLK):
                    values(0, 0, i)
                gate_logits(0)
                gates(0)
                for c in range(4):
                    add_ffn(0, 0, c)
                for m in range(NMAX):
                    reduce_bank(0, 0, m)
                row_max(0, 0)
                max_parts(misc_count(None, "MT", -1), 0, 0)

            def period(b, par):
                for s in range(SLOTS):
                    g, r = divmod(s, NREG)
                    banks = max_banks(b, s)
                    for m in banks[0:2]:
                        reduce_bank(*next_quad(b, g), m)
                    for kind, idx in tasks_at(b, s):
                        if kind == "O":
                            add_attention(misc_count(b, "O", idx), b - 1, 1 - par, idx)
                        elif kind == "stats":
                            statistics(b + 1, idx)
                        elif kind == "norm":
                            normalise(b + 1, idx)
                        elif kind == "QK":
                            rotate(b + 1, idx)
                        elif kind == "V":
                            values(b + 1, 1 - par, idx)
                        elif kind == "gate_logits":
                            gate_logits(b + 1)
                        elif kind == "gates":
                            gates(b + 1)
                        elif kind == "F":
                            add_ffn(b + 1, 1 - par, idx)
                    for m in banks[2:]:
                        reduce_bank(*next_quad(b, g), m)
                    if banks and banks[-1] == NMAX - 1:
                        row_max(*next_quad(b, g))
                    if r == 6:
                        if g > 0:
                            invert_sums(b, g - 1)
                        elif not is_zero(b):
                            invert_sums(b - 1, QUADS - 1)
                    if r == MT_SLOT and has_max(b, s):
                        max_parts(misc_count(b, "MT", g), *next_quad(b, g))

            def end():
                invert_sums(B - 1, QUADS - 1)
                for c in range(4):
                    add_attention(END_BASE + c, B - 1, 1, c)

            run_periods(dve, first, period, end)

        @block.gpsimd
        def _(pool):
            def inverse_deviation(bn, c):
                blocks = slice(2 * c, 2 * c + 2)
                wait_alone(pool, mv_ready, bn * 4 + c + 1)
                nc.gpsimd.tensor_scalar(veps[:, blocks], mv[:, blocks, 1], EPS, None, ALU.add).then_inc(rstd_steps, 1)
                pool.wait_ge(rstd_steps, bn * 8 + c * 2 + 1)
                nc.gpsimd.tensor_tensor(rstd[:, blocks], veps[:, blocks], minus_half[:, blocks], ALU.pow).then_inc(rstd_steps, 1)

            def add_biases(bn, par):
                pool.wait_ge(x_landed[par], bn * 8 + (8 if par else 16))
                for i in range(BLK):
                    last = nc.gpsimd.tensor_tensor(x[par][:, i, :], x[par][:, i, :], bo[:], ALU.add)
                last.then_inc(xb_ready, 1)

            def rotated(bn, u):
                pool.wait_ge(rot_in, bn * 8 + u * 2 + 2)
                pool.wait_ge(misc_drained, misc_of(bn, "QK", 2 * u + 1) + 1)
                nc.gpsimd.tensor_tensor(rot[:, 0, :], rot[:, 0, :], rot[:, 1, :], ALU.subtract).then_inc(rot_steps, 1)
                pool.wait_ge(rot_steps, bn * 16 + u * 4 + 1)
                nc.gpsimd.tensor_tensor(rot[:, 1, :], rot[:, 2, :], rot[:, 3, :], ALU.add).then_inc(rot_steps, 1)
                pool.wait_ge(rot_steps, bn * 16 + u * 4 + 2)

            def left_over(bn, u, n):
                pool.wait_ge(cast_steps, bn * 8 + u * 2 + n + 1)
                for e in range(2):
                    dst = rot[:, 2 + e, :] if n == 0 else parts[:, 2, e, :]
                    last = nc.gpsimd.tensor_tensor(dst, rot[:, 2 * n + e, :], parts[:, n, e, :], ALU.subtract)
                last.then_inc(rot_steps, 1)

            def mask_region(b, g, r):
                kind = REGIONS[r][0]
                wait_alone(pool, exped, b * SLOTS + g * NREG + r + 1)
                tile_ = pt[(g * NREG + r) % PT_RING]
                n = QH if kind == "C" else 2
                heads = tile_[:, :].rearrange("p (h w) -> p h w", h=n)
                for at in (0, 3 * P) if kind == "B" else (0,):
                    blocks = heads[:, :, at:at + P]
                    last = nc.gpsimd.affine_select(out=blocks, in_=blocks, compare_op=ALU.is_ge, fill=0.0, base=0, pattern=[[0, n], [1, P]],
                                                   channel_multiplier=-1)
                last.then_inc(masked, 1)

            def scale_heads(b, hh):
                pool.wait_ge(sc_landed, (b * QUADS + 2 * hh + 2) * 64)
                for n in range(2):
                    for half in range(2):
                        pool.wait_ge(halves_landed[half], (b * QUADS + 2 * hh + 2) * 128)
                    cols = slice(n * HALF, (n + 1) * HALF)
                    last = nc.gpsimd.tensor_tensor(oc[:, hh, cols], oc[:, hh, cols], sc[:, cols], ALU.mult)
                last.then_inc(attn_ready, 1)

            def first():
                nc.gpsimd.memset(minus_half[:], -0.5)
                nc.gpsimd.memset(identf[:], 0.0)
                nc.gpsimd.memset(identb[:], 0.0)
                nc.gpsimd.memset(maskb[:], 0.0).then_inc(pool_steps, 1)
                pool.wait_ge(pool_steps, 1)
                for m in (identf, identb):
                    nc.gpsimd.affine_select(out=m[:], in_=m[:], compare_op=ALU.not_equal, fill=1.0, base=0, pattern=[[-1, P]], channel_multiplier=1)
                nc.gpsimd.affine_select(out=maskb[:], in_=maskb[:], compare_op=ALU.is_ge, fill=MASKED, base=0, pattern=[[-1, P]],
                                        channel_multiplier=1).then_inc(ident_ready, 1)
                pool.wait_ge(weights_landed, 16 * 11)
                nc.gpsimd.tensor_tensor(bo[:], bo[:], bb[:], ALU.add).then_inc(bias_ready, 1)
                pool.wait_ge(bias_ready, 1)
                for c in range(4):
                    inverse_deviation(0, c)
                add_biases(0, 0)
                for u in range(4):
                    rotated(0, u)
                    left_over(0, u, 0)
                    left_over(0, u, 1)

            def period(b, par):
                for s in range(SLOTS):
                    g, r = divmod(s, NREG)
                    if r in MASK_REGIONS:
                        mask_region(b, g, r)
                    if r == 10 and g == 2:
                        scale_heads(b, 0)
                    if r == 10 and g == 0 and not is_zero(b):
                        scale_heads(b - 1, 1)
                    for kind, idx in tasks_at(b, s):
                        if kind == "stats":
                            inverse_deviation(b + 1, idx)
                        elif kind == "bias":
                            add_biases(b + 1, 1 - par)
                        elif kind == "rotated":
                            rotated(b + 1, idx)
                        elif kind == "left0":
                            left_over(b + 1, idx, 0)
                        elif kind == "left1":
                            left_over(b + 1, idx, 1)

            def end():
                scale_heads(B - 1, 1)

            run_periods(pool, first, period, end)


_INS = ["x_in", "wqk_in", "bqk_in", "wv_in", "bv_in", "base_in", "wout_in", "lora_in", "bo_in", "bb_in", "cos_in", "sin_in"]


def kernel(**inputs):
    import numpy as np
    import concourse.bacc as bacc
    from concourse.bass_utils import run_bass_kernel_spmd

    def rows_of(a):
        return a.reshape(KD, P, -1).transpose(1, 0, 2)

    w = np.asarray(inputs["L0_attn_w_qkv"])
    b = np.asarray(inputs["L0_attn_b_qkv"])
    w_pairs = w[:2 * D].reshape(2, H, DH // 2, 2, D).transpose(0, 3, 1, 2, 4).reshape(4, P, D)
    b_pairs = b[:2 * D].reshape(2, H, DH // 2, 2).transpose(0, 3, 1, 2).reshape(4, P)
    inv_freq = (1.0 / np.float32(10000.0) ** (np.arange(0, DH, 2, dtype=np.float32) / np.float32(DH))).astype(np.float32)
    angle = np.tile(inv_freq, H)[:, None] * np.arange(T, dtype=np.float32)[None, :]
    wv = np.concatenate([w[2 * D:].T, np.asarray(inputs["L0_ffn_lora_A"]), np.asarray(inputs["L0_ffn_router_w"]).T], axis=1)
    bv = np.concatenate([b[2 * D:], np.zeros(R, np.float32), np.asarray(inputs["L0_ffn_router_b"])])
    lora_b = np.asarray(inputs["L0_ffn_lora_B"]).reshape(E * R, D)
    arrays = {
        "x_in": np.asarray(inputs["L0_attn_x"]),
        "wqk_in": w_pairs.reshape(4, P, KD, P).transpose(3, 2, 0, 1),
        "bqk_in": b_pairs.T,
        "wv_in": rows_of(wv),
        "bv_in": np.broadcast_to(bv, (P, D + NML)),
        "base_in": rows_of(np.asarray(inputs["L0_ffn_base_w"]).T),
        "wout_in": rows_of(np.asarray(inputs["L0_attn_w_out"]).T),
        "lora_in": np.stack([np.concatenate([lora_b, np.zeros_like(lora_b)]), np.concatenate([np.zeros_like(lora_b), lora_b])], axis=1),
        "bo_in": np.broadcast_to(np.asarray(inputs["L0_attn_b_out"]), (P, D)),
        "bb_in": np.broadcast_to(np.asarray(inputs["L0_ffn_base_b"]), (P, D)),
        "cos_in": np.cos(angle).astype(np.float32),
        "sin_in": np.sin(angle).astype(np.float32),
    }
    nc = bacc.Bacc("TRN2", target_bir_lowering=False, num_devices=1)
    given, args = {}, []
    for name in _INS:
        a = np.ascontiguousarray(arrays[name])
        given[f"{name}_dram"] = a
        args.append(nc.dram_tensor(f"{name}_dram", a.shape, mybir.dt.from_np(a.dtype), kind="ExternalInput").ap())
    args.append(nc.dram_tensor("out_dram", (B, T, D), mybir.dt.float32, kind="ExternalOutput").ap())
    attention_ffn_block(nc, *args)
    r = run_bass_kernel_spmd(nc, [given], core_ids=[0])
    return r.results[0]["out_dram"]
```

```python
from contextlib import ExitStack

import concourse.bass as bass
from concourse import mybir

B, T, D, H, DH = 16, 1024, 256, 16, 16
E, R = 8, 8
SCALING = 2.0
EPS = 1e-5
SCORE_SCALE = DH ** -0.5
P = 128
BLK = T // P
KD = D // P
HALF = T // 2
QH = 4
QUADS = H // QH
VC = DH + 1
NML = R + E
PARTS = 3
STACK = 6 * DH
STACK_DMAS = 6
MROWS = STACK + PARTS
Q_PART_ROW, K_PART_ROW = (2, 1, 0), (0, 1, 2)
MASKED = -1e30

REGIONS = []
PV_UNITS = []
for _half in range(2):
    for _kind, _j in [("A", j) for j in range(4 * _half + 1)] + [("B", 4 * _half + 1), ("C", 4 * _half + 2)]:
        _n = 1 if _kind == "C" else 2
        PV_UNITS.append((_half, _kind, _j, list(range(len(REGIONS), len(REGIONS) + _n))))
        REGIONS += [(_kind, _half, _j, 2 * a) for a in range(_n)]
NREG = len(REGIONS)
SLOTS = NREG * QUADS
MASK_REGIONS = [r for r, (kind, half, j, _) in enumerate(REGIONS) if j >= 4 * half]
EXP_RING, MAX_RING = 3, 3
PT_RING = 12
LAG = 3
PV_AT = [(u[3][-1] + LAG) % NREG for u in PV_UNITS]
HALF_END = [max(u[3][-1] for u in PV_UNITS if u[0] == h) for h in range(2)]

MAX_BANKS = []
for _i in range(BLK):
    _c0 = min(_i + 1, 4) * P
    _n = min(QH, HALF // _c0)
    MAX_BANKS += [(_i, 0, 0, _c0, list(range(a, a + _n))) for a in range(0, QH, _n)]
    if _i >= 4:
        _c1 = (_i - 3) * P
        _n = min(QH, HALF // _c1)
        MAX_BANKS += [(_i, 1, HALF, _c1, list(range(a, a + _n))) for a in range(0, QH, _n)]
NMAX = len(MAX_BANKS)
assert 2 * NREG % PT_RING == 0 and 2 * NREG % EXP_RING == 0

TASKS = [
    (0, "load_ln", 0), (0, "load_ln", 1), (2, "stack3", 3), (2, "stats", 0), (4, "norm", 0), (4, "stats", 1),
    (5, "load_ln", 2), (6, "T", 0), (6, "norm", 1), (7, "stats", 2), (9, "load_ln", 3), (9, "norm", 2), (9, "stats", 3),
    (9, "T", 1), (10, "T", 2), (11, "norm", 3), (12, "O", 0), (13, "T", 3), (15, "O", 1), (15, "store", 0), (15, "store", 1),
    (16, "O", 2), (18, "store", 2), (18, "O", 3), (18, "store", 3), (19, "QK", 0), (20, "V", 0), (21, "QK", 1),
    (22, "rotated", 0), (23, "part0", 0), (24, "left0", 0), (24, "V", 1), (25, "left1", 0), (25, "part1", 0), (26, "write", 0),
    (26, "V", 2), (27, "QK", 2), (27, "load_x", 0), (28, "QK", 3), (28, "rotated", 1), (29, "V", 3), (29, "left0", 1),
    (30, "part0", 1), (32, "left1", 1), (32, "part1", 1), (33, "write", 1), (33, "V", 4), (34, "QK", 4), (35, "QK", 5),
    (35, "bias", 0), (36, "rotated", 2), (37, "left0", 2), (37, "part0", 2), (39, "left1", 2), (39, "part1", 2), (39, "V", 5),
    (39, "write", 2), (39, "bias", 1), (41, "QK", 6), (41, "rotated", 3), (42, "QK", 7), (43, "bias", 2), (44, "V", 6),
    (44, "left0", 3), (44, "part0", 3), (44, "bias", 3), (45, "left1", 3), (46, "part1", 3), (46, "V", 7), (47, "write", 3),
    (47, "gate_logits", 0), (48, "gate_exp", 0), (49, "gates", 0), (50, "stack", 0), (50, "stack", 1), (51, "GT", 0),
    (52, "F", 0), (54, "F", 1), (58, "stack", 2), (68, "F", 2), (70, "F", 3),
]
MAX_COUNTS = (
    3, 3, 1, 3, 3, 3, 0, 2, 4, 3, 4, 3, 4, 2, 1, 1, 2, 4,
    1, 1, 4, 3, 2, 3, 3, 1, 4, 1, 3, 3, 1, 1, 2, 1, 2, 2,
    2, 3, 4, 2, 4, 1, 2, 1, 3, 2, 2, 2, 2, 0, 0, 0, 0, 0,
    0, 2, 1, 3, 4, 1, 3, 1, 2, 3, 3, 5, 2, 4, 4, 0, 0, 0,
)
MT_AT = (14, 31, 49, 69)
assert sum(MAX_COUNTS) == QUADS * NMAX and all(sum(MAX_COUNTS[:s]) == (g + 1) * NMAX for g, s in enumerate(MT_AT))
MAX_AT = []
for _s, _n in enumerate(MAX_COUNTS):
    _g, _m = divmod(sum(MAX_COUNTS[:_s]), NMAX)
    MAX_AT.append((min(_g, QUADS - 1), range(_m, _m + _n) if _n else range(0)))
BANK_KINDS = ("O", "T", "QK", "V", "GT", "F", "MT")
MTS = [(s, "MT", g) for g, s in enumerate(MT_AT)]
BANK_ORDER = [(k, i) for s, k, i in sorted(TASKS + MTS, key=lambda x: (x[0], x[1] == "MT")) if k in BANK_KINDS]
NBANK = len(BANK_ORDER)
PERIOD0_ORDER = [x for x in BANK_ORDER if x[0] != "O"]
LAST_ORDER = [x for x in BANK_ORDER if x[0] == "O" or x in [("MT", g) for g in range(QUADS - 1)]]
FIRST_ORDER = [("T", c) for c in range(4)] + [("QK", 0), ("QK", 1), ("V", 0), ("V", 1), ("V", 2), ("QK", 2), ("QK", 3)]
FIRST_ORDER += [("V", i) for i in (3, 4, 5)] + [("QK", 4), ("QK", 5), ("V", 6), ("V", 7), ("QK", 6), ("QK", 7), ("GT", 0)]
FIRST_ORDER += [("F", c) for c in range(4)] + [("MT", -1)]
NFIRST = len(FIRST_ORDER)
END_BASE = NFIRST - 4 + NBANK * (B - 1) + len(LAST_ORDER)
BOTH_FREE = (4, FIRST_ORDER.index(("GT", 0)), FIRST_ORDER.index(("GT", 0)) + 1, END_BASE)


def attention_ffn_block(nc, x_in, wqk_in, bqk_in, wv_in, bv_in, base_in, wout_in, lora_in, bo_in, bb_in, cos_in, sin_in, out):
    f32, bf16 = mybir.dt.float32, mybir.dt.bfloat16
    ALU, ACT, AX = mybir.AluOpType, mybir.ActivationFunctionType, mybir.AxisListType.X

    x_blocks = x_in.rearrange("b (n p) d -> b p n d", p=P)
    out_blocks = out.rearrange("b (n p) d -> b p n d", p=P)
    parts_dram = [nc.dram_tensor(f"parts{n}_dram", (2, H, PARTS, DH, T), bf16, kind="Internal").ap() for n in range(2)]
    rsum_dram = nc.dram_tensor("rsum_dram", (2, QH, HALF), f32, kind="Internal").ap()

    with ExitStack() as ctx:
        def sb(name, shape, dt=f32):
            return ctx.enter_context(nc.sbuf_tensor(name, shape, dt))

        def sem(name):
            return ctx.enter_context(nc.semaphore(name))

        wqk = sb("wqk", [P, KD, 4, P])
        bqk = sb("bqk", [P, 4])
        wv = sb("wv", [P, KD, D + NML])
        bv = sb("bv", [P, D + NML])
        base = sb("base", [P, KD, D])
        wout = sb("wout", [P, KD, D])
        lora = sb("lora", [P, 2, D])
        bo = sb("bo", [P, D])
        bb = sb("bb", [P, D])
        cos = sb("cos", [P, T])
        sin = sb("sin", [P, T])
        identf = sb("identf", [P, P])
        identb = sb("identb", [P, P], bf16)
        maskb = sb("maskb", [P, P], bf16)
        minus_half = sb("minus_half", [P, BLK])
        x = [sb(f"x{n}", [P, BLK, D]) for n in range(2)]
        x_ln = [sb(f"x_ln{n}", [P, 2, D]) for n in range(2)]
        xn = [sb(f"xn{n}", [P, 2, D]) for n in range(2)]
        xnT = sb("xnT", [P, KD, T])
        bst = sb("bst", [P, BLK, 6])
        mv = sb("mv", [P, BLK, 2])
        veps = sb("veps", [P, BLK])
        rstd = sb("rstd", [P, BLK])
        rots = [sb(f"rot{n}", [P, 4, HALF]) for n in range(2)]
        parts = sb("parts", [P, PARTS, 2, HALF], bf16)
        qs = [sb(f"qs{g}", [MROWS, QH, T], bf16) for g in range(QUADS)]
        ks = [sb(f"ks{g}", [MROWS, QH, T], bf16) for g in range(QUADS)]
        v_aug = [sb(f"v_aug{n}", [P, BLK, H, VC]) for n in range(2)]
        ml = sb("ml", [P, BLK, NML])
        gmax = sb("gmax", [P, BLK])
        glog = sb("glog", [P, BLK, E])
        gexp = sb("gexp", [P, BLK, E])
        gsum = sb("gsum", [P, BLK])
        gate = sb("gate", [P, BLK, E], bf16)
        gm = sb("gm", [P, BLK, E, R])
        gmT = sb("gmT", [P, BLK // 2, P])
        pmax = sb("pmax", [P, QH, BLK, 2])
        rmax = sb("rmax", [P, QH, BLK])
        mres = sb("mres", [QH * BLK, P])
        mrow = sb("mrow", [QH * BLK, PARTS, P], bf16)
        pt = [sb(f"pt{n}", [P, HALF]) for n in range(PT_RING)]
        oev = sb("oev", [P, 2, HALF])
        su = sb("su", [QH * BLK, P])
        su_inv = sb("su_inv", [QH * BLK, P])
        oc = sb("oc", [P, 2, T])
        sc = sb("sc", [P, T])

        exp_ps = [ctx.enter_context(nc.psum_tensor(f"exp_ps{n}", [P, HALF], f32)) for n in range(EXP_RING)]
        max_ps = [ctx.enter_context(nc.psum_tensor(f"max_ps{n}", [P, HALF], f32)) for n in range(MAX_RING)]
        pv_ps = ctx.enter_context(nc.psum_tensor("pv_ps", [P, HALF], f32))
        misc = ctx.enter_context(nc.psum_tensor("misc", [P, HALF], f32))

        qk_weights_landed = sem("qk_weights_landed")
        weights_landed = sem("weights_landed")
        ident_ready = sem("ident_ready")
        consts_ready = sem("consts_ready")
        bias_ready = sem("bias_ready")
        pool_steps = sem("pool_steps")
        x_landed = [sem(f"x_landed{n}") for n in range(2)]
        mv_ready = sem("mv_ready")
        stat_steps = sem("stat_steps")
        rstd_steps = sem("rstd_steps")
        xn_ready = sem("xn_ready")
        xb_ready = sem("xb_ready")
        misc_filled = sem("misc_filled")
        misc_drained = sem("misc_drained")
        rot_in = sem("rot_in")
        rot_steps = sem("rot_steps")
        cast_steps = sem("cast_steps")
        parts_landed = sem("parts_landed")
        stack_landed = [sem(f"stack_landed{g}") for g in range(QUADS)]
        rows_landed = [sem(f"rows_landed{g}") for g in range(QUADS)]
        v_ready = sem("v_ready")
        gate_steps = sem("gate_steps")
        gate_exp = sem("gate_exp")
        max_scored = sem("max_scored")
        max_reduced = sem("max_reduced")
        quad_steps = sem("quad_steps")
        rmax_ready = sem("rmax_ready")
        mrow_ready = sem("mrow_ready")
        scored = sem("scored")
        exped = sem("exped")
        masked = sem("masked")
        pv_done = sem("pv_done")
        evacuated = sem("evacuated")
        halves_landed = [sem(f"halves_landed{n}") for n in range(2)]
        recip_ready = sem("recip_ready")
        rsum_landed = sem("rsum_landed")
        sc_landed = sem("sc_landed")
        attn_ready = sem("attn_ready")
        ln_landed = [sem(f"ln_landed{n}") for n in range(2)]
        stored = sem("stored")

        block = ctx.enter_context(nc.Block())

        NHALF = 2 * NREG
        DIAG = 2 * len(MASK_REGIONS)

        def misc_count(b, kind, idx):
            if b is None:
                return FIRST_ORDER.index((kind, idx))
            if is_zero(b):
                return NFIRST + PERIOD0_ORDER.index((kind, idx))
            order = LAST_ORDER if isinstance(b, int) and b == B - 1 else BANK_ORDER
            return NFIRST - 4 + NBANK * b + order.index((kind, idx))

        def misc_of(bb_, kind, idx):
            return misc_count(None, kind, idx) if isinstance(bb_, int) and bb_ == 0 else misc_count(bb_ - 1, kind, idx)

        def two_banks(n):
            return isinstance(n, int) and (n < NFIRST - 1 or n >= END_BASE)

        def bank_of(n):
            return exp_ps[0] if two_banks(n) and n % 2 == 1 else misc

        def is_zero(v):
            return isinstance(v, int) and v == 0

        def wait_alone(eng, semaphore, count):
            if not isinstance(count, int):
                count = eng.to_reg(count)
            eng.wait_ge(ident_ready, 1)
            eng.wait_ge(semaphore, count)

        def run_periods(eng, first, period, end):
            first()
            period(0, 0)
            with eng.Fori(0, (B - 2) // 2) as i:
                period(i * 2 + 1, 1)
                period(i * 2 + 2, 0)
            period(B - 1, 1)
            end()

        def tasks_at(b, s):
            for slot, kind, idx in TASKS:
                if slot == s:
                    if kind in ("O", "store") and is_zero(b):
                        continue
                    if kind not in ("O", "store", "stack3") and isinstance(b, int) and b == B - 1:
                        continue
                    yield kind, idx

        def has_next(b, g):
            return not (isinstance(b, int) and b == B - 1 and g == QUADS - 1)

        def next_quad(b, g):
            return (b, g + 1) if g < QUADS - 1 else (b + 1, 0)

        def max_before_misc(b, s):
            return 2 + (s % NREG in PV_AT) + any(k in ("O", "QK", "F") for k, _ in tasks_at(b, s))

        def max_banks(b, s):
            return MAX_AT[s][1] if has_next(b, MAX_AT[s][0]) else range(0)

        def normalise(eng, ops, bn, c):
            if not (is_zero(bn) and c < 2):
                n = misc_of(bn, "T", c - 2) if c >= 2 else misc_of(bn - 1, "F", 3)
                wait_alone(eng, misc_filled, n + 1)
            wait_alone(eng, rstd_steps, bn * 8 + c * 2 + 2)
            for m in range(2):
                i = 2 * c + m
                last = ops.tensor_scalar(xn[c % 2][:, m, :], x_ln[c % 2][:, m, :], mv[:, i, 0:1], rstd[:, i:i + 1], ALU.subtract, ALU.mult)
            last.then_inc(xn_ready, 1)

        def rotated(eng, ops, bn, u):
            rot = rots[u % 2]
            eng.wait_ge(rot_in, bn * 8 + u * 2 + 2)
            eng.wait_ge(misc_drained, misc_of(bn, "QK", 2 * u + 1) + 1)
            ops.tensor_tensor(rot[:, 0, :], rot[:, 0, :], rot[:, 1, :], ALU.subtract).then_inc(rot_steps, 1)
            eng.wait_ge(rot_steps, bn * 16 + u * 4 + 1)
            ops.tensor_tensor(rot[:, 1, :], rot[:, 2, :], rot[:, 3, :], ALU.add).then_inc(rot_steps, 1)
            eng.wait_ge(rot_steps, bn * 16 + u * 4 + 2)

        def left_over(eng, ops, bn, u, n):
            rot = rots[u % 2]
            eng.wait_ge(cast_steps, bn * 8 + u * 2 + n + 1)
            for e in range(2):
                dst = rot[:, 2 + e, :] if n == 0 else parts[:, 2, e, :]
                last = ops.tensor_tensor(dst, rot[:, 2 * n + e, :], parts[:, n, e, :], ALU.subtract)
            last.then_inc(rot_steps, 1)

        @block.sync
        def _(sp):
            def load_x(bn, par):
                if not is_zero(bn) and not (isinstance(bn, int) and bn == 1):
                    wait_alone(sp, stored, 64 * (bn - 1))
                sp.dma_start(x[par][:], x_blocks[bn]).then_inc(x_landed[par], 16)

            def load_ln(bn, c):
                if not (is_zero(bn) and c < 2):
                    wait_alone(sp, xn_ready, bn * 4 + c - 1)
                sp.dma_start(x_ln[c % 2][:], x_blocks[bn][:, 2 * c:2 * c + 2, :]).then_inc(ln_landed[c % 2], 16)

            def store(n, bp, par, c):
                wait_alone(sp, misc_drained, n + 1)
                sp.dma_start(out_blocks[bp][:, 2 * c:2 * c + 2, :], x[par][:, 2 * c:2 * c + 2, :]).then_inc(stored, 16)

            def write_parts(bn, par, u):
                qk, half = u // 2, u % 2
                wait_alone(sp, rot_steps, bn * 16 + u * 4 + 4)
                dst = parts_dram[par][qk].rearrange("h p (d e) t -> p h d e t", e=2)[:, :, :, :, half * HALF:(half + 1) * HALF]
                for n in range(PARTS):
                    row = (Q_PART_ROW, K_PART_ROW)[qk][n]
                    sp.dma_start(dst[row], parts[:, n]).then_inc(parts_landed, 16)

            def load_stack(bn, par, g):
                wait_alone(sp, parts_landed, (bn + 1) * 16 * 4 * PARTS)
                if not is_zero(bn):
                    wait_alone(sp, scored, bn * (2 * SLOTS) - 2 * SLOTS + NHALF * (g + 1))
                for st, qk in ((qs[g], 0), (ks[g], 1)):
                    src = parts_dram[par][qk, g * QH:(g + 1) * QH].rearrange("h p r t -> (p r) h t")
                    for row, first_part, last_part in ((0, 0, PARTS), (3 * DH, 1 - qk, PARTS - qk), (5 * DH, 2 - 2 * qk, 3 - 2 * qk)):
                        sp.dma_start(st[row:row + (last_part - first_part) * DH, :, :], src[first_part * DH:last_part * DH]).then_inc(stack_landed[g], 16)

            def max_rows(bt, g):
                wait_alone(sp, mrow_ready, bt * QUADS + g + 1)
                for c in range(PARTS):
                    sp.dma_start(qs[g][STACK + c:STACK + c + 1, :, :], mrow[:, c, :]).then_inc(rows_landed[g], 16)

            def half_out(b, g, half):
                hh = g // 2
                if half == 0 and g % 2 == 0:
                    if not (is_zero(b) and hh == 0):
                        if not is_zero(b):
                            wait_alone(sp, misc_filled, misc_count(b, "O", 3) + 1)
                wait_alone(sp, evacuated, b * 8 + g * 2 + half + 1)
                if half == 0 and not (is_zero(b) and g == 0):
                    wait_alone(sp, recip_ready, b * QUADS + g)
                for a in range(QH):
                    row = (g % 2 * QH + a) * DH
                    sp.dma_start(oc[row:row + DH, hh, half * HALF:(half + 1) * HALF], oev[32 * a:32 * a + DH, half, :]).then_inc(halves_landed[half], 16)
                sp.dma_start(su[half * QH * BLK // 2:(half + 1) * QH * BLK // 2, :],
                             oev[DH:P:32, half, :]).then_inc(halves_landed[half], 16)

            def sums_out(b, g):
                q = b * QUADS + g
                wait_alone(sp, recip_ready, q + 1)
                if not (is_zero(b) and g == 0):
                    wait_alone(sp, sc_landed, q * 32)
                sp.dma_start(rsum_dram.rearrange("f a (c t) -> (f a c) t", t=P), su_inv[:, :]).then_inc(rsum_landed, 16)
                wait_alone(sp, rsum_landed, (q + 1) * 16)
                if g % 2 == 0 and not (is_zero(b) and g == 0):
                    wait_alone(sp, attn_ready, b * 2 + g // 2)
                row = g % 2 * QH * DH
                for half in range(2):
                    sp.dma_start(sc[row:row + QH * DH, half * HALF:(half + 1) * HALF],
                                 rsum_dram[half].unsqueeze(1).broadcast_to([QH, DH, HALF])).then_inc(sc_landed, 16)

            def first():
                load_ln(0, 0)
                load_ln(0, 1)
                for dst, src in ((wqk, wqk_in), (bqk, bqk_in), (cos, cos_in), (sin, sin_in)):
                    sp.dma_start(dst[:], src).then_inc(qk_weights_landed, 16)
                load_ln(0, 2)
                load_ln(0, 3)
                for dst, src in ((wv, wv_in), (bv, bv_in), (bo, bo_in), (bb, bb_in), (base, base_in), (lora, lora_in), (wout, wout_in)):
                    sp.dma_start(dst[:], src).then_inc(weights_landed, 16)
                load_x(0, 0)
                load_x(1, 1)
                for u in range(4):
                    write_parts(0, 0, u)
                for g in range(3):
                    load_stack(0, 0, g)
                max_rows(0, 0)

            def period(b, par):
                for s in range(SLOTS):
                    g, r = divmod(s, NREG)
                    if g == 0 and r == 3 and not is_zero(b):
                        half_out(b - 1, QUADS - 1, 1)
                    if g == 0 and r == 7 and not is_zero(b):
                        sums_out(b - 1, QUADS - 1)
                    if g > 0 and r == 3:
                        half_out(b, g - 1, 1)
                    if g > 0 and r == 7:
                        sums_out(b, g - 1)
                    if r == 9 and g > 0:
                        half_out(b, g, 0)
                    if g == 1 and r == 1:
                        half_out(b, 0, 0)
                    for kind, idx in tasks_at(b, s):
                        if kind == "stack3":
                            load_stack(b, par, 3)
                        elif kind == "stack":
                            load_stack(b + 1, 1 - par, idx)
                        elif kind == "load_ln":
                            load_ln(b + 1, idx)
                        elif kind == "load_x" and not is_zero(b):
                            load_x(b + 1, 1 - par)
                        elif kind == "store":
                            store(misc_count(b, "O", idx), b - 1, 1 - par, idx)
                        elif kind == "write":
                            write_parts(b + 1, 1 - par, idx)
                    if s in MT_AT and has_next(b, MT_AT.index(s)):
                        max_rows(*next_quad(b, MT_AT.index(s)))

            def end():
                half_out(B - 1, QUADS - 1, 1)
                sums_out(B - 1, QUADS - 1)
                for c in range(4):
                    store(END_BASE + c, B - 1, 1, c)
                wait_alone(sp, stored, 64 * B)
                wait_alone(sp, rsum_landed, 16 * QUADS * B)
                wait_alone(sp, parts_landed, 16 * 4 * PARTS * B)

            run_periods(sp, first, period, end)

        @block.tensor
        def _(pe):
            def bank_free(n):
                two = two_banks(n) and n not in BOTH_FREE
                if not (isinstance(n, int) and n < (2 if two else 1)):
                    pe.wait_ge(misc_drained, n - 1 if two else n)

            def nothing():
                pass

            def transposes(bn, c):
                bank_free(misc_of(bn, "T", c))
                bank = bank_of(misc_of(bn, "T", c))
                pe.wait_ge(xn_ready, bn * 4 + c + 1)
                for k in range(KD):
                    for m in range(2):
                        last = nc.tensor.transpose(bank[:, k * 256 + m * P:k * 256 + (m + 1) * P], xn[c % 2][:, m, k * P:(k + 1) * P], identf[:])
                last.then_inc(misc_filled, 1)

            def project_qk(bn, u, between=nothing):
                bank_free(misc_of(bn, "QK", u))
                bank = bank_of(misc_of(bn, "QK", u))
                tile_, half = 2 * (u // 4) + u % 2, u // 2 % 2
                for k in range(KD):
                    last = nc.tensor.matmul(bank[:, :], wqk[:, k, tile_, :], xnT[:, k, half * HALF:(half + 1) * HALF], start=(k == 0), stop=(k == KD - 1))
                    if k == 0:
                        between()
                last.then_inc(misc_filled, 1)

            def project_v(bn, i):
                bank_free(misc_of(bn, "V", i))
                bank = bank_of(misc_of(bn, "V", i))
                for k in range(KD):
                    last = nc.tensor.matmul(bank[:, 0:D + NML], xnT[:, k, i * P:(i + 1) * P], wv[:, k, :], start=(k == 0), stop=(k == KD - 1))
                last.then_inc(misc_filled, 1)

            def transpose_gates(bn):
                bank_free(misc_of(bn, "GT", 0))
                bank = bank_of(misc_of(bn, "GT", 0))
                pe.wait_ge(gate_steps, bn * 6 + 6)
                for c in range(BLK // 2):
                    last = nc.tensor.transpose(bank[:, c * P:(c + 1) * P], gm[:, 2 * c:2 * c + 2, :, :].rearrange("p n e r -> p (n e r)"), identf[:])
                last.then_inc(misc_filled, 1)

            def ffn(bn, c, between=nothing):
                bank_free(misc_of(bn, "F", c))
                bank = bank_of(misc_of(bn, "F", c))
                for m in range(2):
                    dst, i = bank[:, m * D:(m + 1) * D], 2 * c + m
                    for k in range(KD):
                        nc.tensor.matmul(dst, xnT[:, k, i * P:(i + 1) * P], base[:, k, :], start=(k == 0), stop=False)
                    last = nc.tensor.matmul(dst, gmT[:, c, :], lora[:, m, :], start=False, stop=True)
                    if m == 0:
                        between()
                last.then_inc(misc_filled, 1)

            def out_product(n, bp, c, between=nothing):
                bank_free(n)
                bank = bank_of(n)
                if c == 0:
                    pe.wait_ge(attn_ready, bp * 2 + 2)
                for m in range(2):
                    i = 2 * c + m
                    for k in range(KD):
                        last = nc.tensor.matmul(bank[:, m * D:(m + 1) * D], oc[:, k, i * P:(i + 1) * P], wout[:, k, :], start=(k == 0), stop=(k == KD - 1))
                    if m == 0:
                        between()
                last.then_inc(misc_filled, 1)

            def transpose_max(n, q):
                bank_free(n)
                pe.wait_ge(rmax_ready, q + 1)
                nc.tensor.transpose(misc[0:QH * BLK, 0:P], rmax[:].rearrange("p h i -> p (h i)"), identf[:]).then_inc(misc_filled, 1)

            def max_bank(bt, g, m):
                i, _, key0, w, heads = MAX_BANKS[m]
                q = bt * QUADS + g
                if m == 0:
                    pe.wait_ge(stack_landed[g], (bt + 1) * STACK_DMAS * 16)
                if not (is_zero(q) and m < MAX_RING):
                    before = m - MAX_RING if m >= MAX_RING else max(n for n in range(NMAX) if n % MAX_RING == m) - NMAX
                    pe.wait_ge(max_reduced, q * NMAX + before + 1)
                bank = max_ps[m % MAX_RING]
                diag = key0 + w == (i + 1) * P
                for n, h in enumerate(heads):
                    last = nc.tensor.matmul(bank[:, n * w:(n + 1) * w], qs[g][0:STACK, h, i * P:(i + 1) * P], ks[g][0:STACK, h, key0:key0 + w], start=True, stop=not diag)
                    if diag:
                        last = nc.tensor.matmul(bank[:, (n + 1) * w - P:(n + 1) * w], identb[:], maskb[:], start=False, stop=True)
                last.then_inc(max_scored, 1)

            def score_bank(b, g, r, a):
                at_quad = 2 * r + a
                n = b * (2 * SLOTS) + g * NHALF + at_quad
                kind, half, j, h0 = REGIONS[r]
                t0 = half * HALF
                if at_quad == 0:
                    pe.wait_ge(rows_landed[g], (b + 1) * 48)
                if not (isinstance(n, int) and n < EXP_RING):
                    pe.wait_ge(exped, n - EXP_RING + 1)
                ps = exp_ps[at_quad % EXP_RING]
                if kind == "A":
                    todo = [(0, h0 + a, j, 0)]
                elif kind == "B":
                    todo = [(0, h0 + a, j, P), (3 * P, h0 + a, j + 2, 3 * P)]
                else:
                    todo = [(h * 2 * P, 2 * a + h, j, 2 * P) for h in range(2)]
                for at, h, jj, f in todo:
                    w = HALF - f
                    last = nc.tensor.matmul(ps[:, at:at + w], ks[g][0:MROWS, h, jj * P:(jj + 1) * P], qs[g][0:MROWS, h, t0 + f:t0 + HALF], start=True, stop=True)
                last.then_inc(scored, 1)

            def pv_unit(b, par, g, unit):
                half, kind, j, regions = unit
                q0 = b * (2 * SLOTS) + g * NHALF
                if regions[0] == 0 and g == 0:
                    pe.wait_ge(v_ready, b * BLK + BLK)
                pe.wait_ge(exped, q0 + 2 * regions[-1] + 2)
                if j >= 4 * half:
                    pe.wait_ge(masked, (b * QUADS + g) * DIAG + 2 * MASK_REGIONS.index(regions[-1]) + 2)
                if j == 0 and not (is_zero(b) and g == 0 and half == 0):
                    pe.wait_ge(evacuated, (b * QUADS + g) * 2 + half)
                for h in range(QH):
                    if kind == "C":
                        src = pt[(2 * regions[0] + h // 2) % PT_RING]
                        todo = [(h % 2 * 2 * P, j, 2 * P)]
                    else:
                        src = pt[(2 * regions[h // 2] + h % 2) % PT_RING]
                        todo = [(0, j, 0)] if kind == "A" else [(0, j, P), (3 * P, j + 2, 3 * P)]
                    for at, jj, f in todo:
                        last = nc.tensor.matmul(pv_ps[32 * h:32 * h + VC, f:HALF], v_aug[par][:, jj, g * QH + h, :], src[:, at:at + HALF - f],
                                                start=(j == 0), stop=(kind == "C"))
                    if kind != "C" or h % 2 == 1:
                        last.then_inc(pv_done, 1)

            def late_pv(b, par, s):
                g, r = divmod(s - LAG, NREG)
                for unit in PV_UNITS:
                    if unit[3][-1] == r:
                        pv_unit(b, par, g, unit)

            def first():
                pe.wait_ge(ident_ready, 1)
                for kind, idx in FIRST_ORDER[:-1]:
                    if kind == "T":
                        transposes(0, idx)
                    elif kind == "QK":
                        if idx == 0:
                            pe.wait_ge(qk_weights_landed, 16 * 4)
                        project_qk(0, idx)
                    elif kind == "V":
                        if idx == 0:
                            pe.wait_ge(weights_landed, 16 * 7)
                        project_v(0, idx)
                    elif kind == "GT":
                        transpose_gates(0)
                    else:
                        ffn(0, idx)
                pe.wait_ge(consts_ready, 1)
                pe.wait_ge(pool_steps, 2)
                for m in range(NMAX):
                    max_bank(0, 0, m)
                transpose_max(misc_count(None, "MT", -1), 0)

            def period(b, par):
                for s in range(SLOTS):
                    g, r = divmod(s, NREG)
                    banks = iter(max_banks(b, s))

                    def one_max():
                        for m in banks:
                            max_bank(*next_quad(b, MAX_AT[s][0]), m)
                            return

                    for a in range(2):
                        score_bank(b, g, r, a)
                        one_max()
                    if s >= LAG:
                        late_pv(b, par, s)
                    elif not is_zero(b):
                        late_pv(b - 1, 1 - par, s + SLOTS)
                    if r in PV_AT:
                        one_max()
                    for kind, idx in tasks_at(b, s):
                        if kind == "O":
                            out_product(misc_count(b, "O", idx), b - 1, idx, one_max)
                        elif kind == "T":
                            transposes(b + 1, idx)
                        elif kind == "QK":
                            project_qk(b + 1, idx, one_max)
                        elif kind == "V":
                            project_v(b + 1, idx)
                        elif kind == "GT":
                            transpose_gates(b + 1)
                        elif kind == "F":
                            ffn(b + 1, idx, one_max)
                    for m in banks:
                        max_bank(*next_quad(b, MAX_AT[s][0]), m)
                    if s in MT_AT and has_next(b, MT_AT.index(s)):
                        transpose_max(misc_count(b, "MT", MT_AT.index(s)), b * QUADS + MT_AT.index(s) + 1)

            def end():
                for s in range(LAG):
                    late_pv(B - 1, 1, SLOTS + s)
                for c in range(4):
                    out_product(END_BASE + c, B - 1, c)

            run_periods(pe, first, period, end)

        @block.scalar
        def _(act):
            def drain_misc(dst, n):
                act.wait_ge(misc_filled, n + 1)
                nc.scalar.activation(dst, bank_of(n)[:, :].rearrange("p (a n) -> p a n", a=dst.shape[1]), ACT.Copy).then_inc(misc_drained, 1)

            def transposed_rows(bn, c):
                drain_misc(xnT[:, :, c * 256:(c + 1) * 256], misc_of(bn, "T", c))

            def transposed_gates(bn):
                drain_misc(gmT[:, :, :], misc_of(bn, "GT", 0))

            def part(bn, u, n):
                if n == 0 and not (is_zero(bn) and u == 0):
                    act.wait_ge(parts_landed, (bn * 4 + u) * 16 * PARTS)
                act.wait_ge(rot_steps, bn * 16 + u * 4 + (2 if n == 0 else 3))
                nc.scalar.activation(parts[:, n, :, :], rots[u % 2][:, 2 * n:2 * n + 2, :], ACT.Copy).then_inc(cast_steps, 1)

            def gate_exps(bn):
                act.wait_ge(gate_steps, bn * 6 + 2)
                nc.scalar.activation(gexp[:], glog[:], ACT.Exp).then_inc(gate_exp, 1)

            def exp_bank(b, g, r, a):
                at_quad = 2 * r + a
                n = b * (2 * SLOTS) + g * NHALF + at_quad
                act.wait_ge(scored, n + 1)
                if not (isinstance(n, int) and n < PT_RING):
                    act.wait_ge(pv_done, n - PT_RING + 1)
                nc.scalar.activation(pt[at_quad % PT_RING][:], exp_ps[at_quad % EXP_RING][:], ACT.Exp, scale=SCORE_SCALE).then_inc(exped, 1)

            def evacuate(b, g, half):
                act.wait_ge(pv_done, b * (2 * SLOTS) + g * NHALF + 2 * HALF_END[half] + 2)
                if not (is_zero(b) and g == 0):
                    act.wait_ge(halves_landed[half], (b * QUADS + g) * 80)
                nc.scalar.activation(oev[:, half, :], pv_ps[:, :], ACT.Copy).then_inc(evacuated, 1)

            def first():
                for c in range(4):
                    transposed_rows(0, c)
                for u in range(4):
                    part(0, u, 0)
                    if u == 3:
                        gate_exps(0)
                    part(0, u, 1)
                transposed_gates(0)

            def period(b, par):
                for s in range(SLOTS):
                    g, r = divmod(s, NREG)
                    for a in range(2):
                        exp_bank(b, g, r, a)
                    if r == LAG + HALF_END[0] + 1:
                        evacuate(b, g, 0)
                    if r == LAG:
                        if g > 0:
                            evacuate(b, g - 1, 1)
                        elif not is_zero(b):
                            evacuate(b - 1, QUADS - 1, 1)
                    for kind, idx in tasks_at(b, s):
                        if kind == "T":
                            transposed_rows(b + 1, idx)
                        elif kind == "GT":
                            transposed_gates(b + 1)
                        elif kind == "part0":
                            part(b + 1, idx, 0)
                        elif kind == "part1":
                            part(b + 1, idx, 1)
                        elif kind == "gate_exp":
                            gate_exps(b + 1)

            def end():
                evacuate(B - 1, QUADS - 1, 1)

            run_periods(act, first, period, end)

        @block.vector
        def _(dve):
            def statistics(bn, c):
                dve.wait_ge(ln_landed[c % 2], bn * 32 + (c // 2) * 16 + 16)
                for m in range(2):
                    last = nc.vector.bn_stats(bst[:, 2 * c + m, :], x_ln[c % 2][:, m, :])
                last.then_inc(stat_steps, 1)
                wait_alone(dve, stat_steps, bn * 4 + c + 1)
                for i in (2 * c, 2 * c + 1):
                    last = nc.vector.bn_aggr(mv[:, i, :], bst[:, i, :])
                last.then_inc(mv_ready, 1)

            def rotate(bn, u):
                unit, eo, half, tile_ = u // 2, u % 2, u // 2 % 2, 2 * (u // 4) + u % 2
                dve.wait_ge(misc_filled, misc_of(bn, "QK", u) + 1)
                bank = bank_of(misc_of(bn, "QK", u))
                rot = rots[unit % 2]
                if eo == 0 and not (is_zero(bn) and unit < 2):
                    dve.wait_ge(rot_steps, bn * 16 + unit * 4 - 4)
                cols = slice(half * HALF, (half + 1) * HALF)
                for dst, table, at_end in ((0 + eo, (cos, sin)[eo], False), (2 + eo, (sin, cos)[eo], True)):
                    last = nc.vector.scalar_tensor_tensor(rot[:, dst, :], bank[:, :], bqk[:, tile_:tile_ + 1], table[:, cols], ALU.add, ALU.mult)
                    if not at_end:
                        last.then_inc(rot_in, 1)
                last.then_inc(misc_drained, 1)

            def values(bn, par, i):
                dve.wait_ge(misc_filled, misc_of(bn, "V", i) + 1)
                bank = bank_of(misc_of(bn, "V", i))
                if i == 0 and not is_zero(bn) and not (isinstance(bn, int) and bn == 1):
                    dve.wait_ge(pv_done, bn * (2 * SLOTS) - 2 * SLOTS)
                nc.vector.tensor_tensor(v_aug[par][:, i, :, 0:DH], bank[:, 0:D].rearrange("p (h d) -> p h d", d=DH),
                                        bv[:, 0:D].rearrange("p (h d) -> p h d", d=DH), ALU.add).then_inc(v_ready, 1)
                nc.vector.tensor_tensor(ml[:, i, :], bank[:, D:D + NML], bv[:, D:D + NML], ALU.add).then_inc(misc_drained, 1)

            def gate_logits(bn):
                dve.wait_ge(misc_drained, misc_of(bn, "V", BLK - 1) + 1)
                logits = ml[:, :, R:NML]
                nc.vector.tensor_reduce(gmax[:], logits, AX, ALU.max).then_inc(gate_steps, 1)
                dve.wait_ge(gate_steps, bn * 6 + 1)
                nc.vector.tensor_tensor(glog[:], logits, gmax[:].unsqueeze(2).broadcast_to([P, BLK, E]), ALU.subtract).then_inc(gate_steps, 1)

            def gates(bn):
                dve.wait_ge(gate_exp, bn + 1)
                nc.vector.tensor_reduce(gsum[:], gexp[:], AX, ALU.add).then_inc(gate_steps, 1)
                dve.wait_ge(gate_steps, bn * 6 + 3)
                nc.vector.reciprocal(gmax[:], gsum[:]).then_inc(gate_steps, 1)
                dve.wait_ge(gate_steps, bn * 6 + 4)
                nc.vector.tensor_tensor(gate[:], gexp[:], gmax[:].unsqueeze(2).broadcast_to([P, BLK, E]), ALU.mult).then_inc(gate_steps, 1)
                dve.wait_ge(gate_steps, bn * 6 + 5)
                for i in range(BLK):
                    last = nc.vector.scalar_tensor_tensor(gm[:, i], gate[:, i].unsqueeze(2).broadcast_to([P, E, R]), SCALING,
                                                          ml[:, i, 0:R].unsqueeze(1).broadcast_to([P, E, R]), ALU.mult, ALU.mult)
                last.then_inc(gate_steps, 1)

            def add_ffn(bn, par, c):
                dve.wait_ge(misc_filled, misc_of(bn, "F", c) + 1)
                bank = bank_of(misc_of(bn, "F", c))
                dve.wait_ge(xb_ready, bn * 4 + c + 1)
                rows = x[par][:, 2 * c:2 * c + 2, :]
                nc.vector.tensor_tensor(rows, bank[:, :].rearrange("p (n d) -> p n d", n=2), rows, ALU.add).then_inc(misc_drained, 1)

            def add_attention(n, bp, par, c):
                dve.wait_ge(misc_filled, n + 1)
                rows = x[par][:, 2 * c:2 * c + 2, :]
                nc.vector.tensor_tensor(rows, bank_of(n)[:, :].rearrange("p (n d) -> p n d", n=2), rows, ALU.add).then_inc(misc_drained, 1)

            def reduce_bank(bt, g, m):
                i, c, _, w, heads = MAX_BANKS[m]
                q = bt * QUADS + g
                dve.wait_ge(max_scored, q * NMAX + m + 1)
                if m == 0 and not is_zero(q):
                    dve.wait_ge(rmax_ready, q)
                nc.vector.tensor_reduce(pmax[:, heads[0]:heads[-1] + 1, i, c], max_ps[m % MAX_RING][:, 0:len(heads) * w].rearrange("p (h w) -> p h w", w=w),
                                        AX, ALU.max).then_inc(max_reduced, 1)

            def row_max(bt, g):
                q = bt * QUADS + g
                dve.wait_ge(max_reduced, (q + 1) * NMAX)
                nc.vector.tensor_tensor(rmax[:], pmax[:, :, :, 0], pmax[:, :, :, 1], ALU.max).then_inc(rmax_ready, 1)

            def max_parts(n, bt, g):
                q = bt * QUADS + g
                dve.wait_ge(misc_filled, n + 1)
                if not is_zero(q):
                    dve.wait_ge(rows_landed[(g - 1) % QUADS], (bt + 1) * 48 if g > 0 else bt * 48)
                neg = misc[0:QH * BLK, 0:P]
                nc.vector.tensor_scalar(mrow[:, 0, :], neg, -1.0, None, ALU.mult).then_inc(quad_steps, 1)
                dve.wait_ge(quad_steps, q * 2 + 1)
                nc.vector.scalar_tensor_tensor(mres[:], neg, -1.0, mrow[:, 0, :], ALU.mult, ALU.subtract).then_inc(misc_drained, 1)
                dve.wait_ge(misc_drained, n + 1)
                nc.vector.tensor_copy(mrow[:, 1, :], mres[:]).then_inc(quad_steps, 1)
                dve.wait_ge(quad_steps, q * 2 + 2)
                nc.vector.tensor_tensor(mrow[:, 2, :], mres[:], mrow[:, 1, :], ALU.subtract).then_inc(mrow_ready, 1)

            def invert_sums(b, g):
                q = b * QUADS + g
                for half in range(2):
                    dve.wait_ge(halves_landed[half], (q + 1) * 80)
                if not (is_zero(b) and g == 0):
                    dve.wait_ge(rsum_landed, q * 16)
                nc.vector.reciprocal(su_inv[:], su[:]).then_inc(recip_ready, 1)

            def first():
                nc.vector.memset(pv_ps[:], 0.0)
                nc.vector.memset(pmax[:], -3e38)
                for n in range(2):
                    nc.vector.memset(v_aug[n][:, :, :, DH:VC], 1.0)
                nc.vector.memset(ks[0][STACK:MROWS, :, :], 1.0).then_inc(consts_ready, 1)
                for c in (0, 2):
                    statistics(0, c)
                    statistics(0, c + 1)
                    normalise(dve, nc.vector, 0, c)
                    normalise(dve, nc.vector, 0, c + 1)
                dve.wait_ge(qk_weights_landed, 16 * 4)
                for kind, idx in FIRST_ORDER:
                    if kind == "QK":
                        if idx % 2 == 0 and idx > 0:
                            left_over(dve, nc.vector, 0, idx // 2 - 1, 1)
                        rotate(0, idx)
                        if idx % 2 == 1:
                            rotated(dve, nc.vector, 0, idx // 2)
                        if idx == 7:
                            gate_logits(0)
                            left_over(dve, nc.vector, 0, 3, 0)
                            gates(0)
                            left_over(dve, nc.vector, 0, 3, 1)
                    elif kind == "V":
                        if idx == 0:
                            dve.wait_ge(weights_landed, 16 * 7)
                        values(0, 0, idx)
                        if idx in (1, 4, 7):
                            left_over(dve, nc.vector, 0, idx // 3, 0)
                    elif kind == "F":
                        add_ffn(0, 0, idx)
                for m in range(NMAX):
                    reduce_bank(0, 0, m)
                row_max(0, 0)
                max_parts(misc_count(None, "MT", -1), 0, 0)

            def period(b, par):
                for s in range(SLOTS):
                    g, r = divmod(s, NREG)
                    banks = max_banks(b, s)
                    first_banks = max_before_misc(b, s)
                    for m in banks[:first_banks]:
                        reduce_bank(*next_quad(b, MAX_AT[s][0]), m)
                    for kind, idx in tasks_at(b, s):
                        if kind == "O":
                            add_attention(misc_count(b, "O", idx), b - 1, 1 - par, idx)
                        elif kind == "stats":
                            statistics(b + 1, idx)
                        elif kind == "QK":
                            rotate(b + 1, idx)
                        elif kind == "V":
                            values(b + 1, 1 - par, idx)
                        elif kind == "gate_logits":
                            gate_logits(b + 1)
                        elif kind == "gates":
                            gates(b + 1)
                        elif kind == "F":
                            add_ffn(b + 1, 1 - par, idx)
                    for m in banks[first_banks:]:
                        reduce_bank(*next_quad(b, MAX_AT[s][0]), m)
                    if NMAX - 1 in banks:
                        row_max(*next_quad(b, MAX_AT[s][0]))
                    if r == 6:
                        if g > 0:
                            invert_sums(b, g - 1)
                        elif not is_zero(b):
                            invert_sums(b - 1, QUADS - 1)
                    if s in MT_AT and has_next(b, MT_AT.index(s)):
                        max_parts(misc_count(b, "MT", MT_AT.index(s)), *next_quad(b, MT_AT.index(s)))

            def end():
                invert_sums(B - 1, QUADS - 1)
                for c in range(4):
                    add_attention(END_BASE + c, B - 1, 1, c)

            run_periods(dve, first, period, end)

        @block.gpsimd
        def _(pool):
            def inverse_deviation(bn, c):
                blocks = slice(2 * c, 2 * c + 2)
                wait_alone(pool, mv_ready, bn * 4 + c + 1)
                nc.gpsimd.tensor_scalar(veps[:, blocks], mv[:, blocks, 1], EPS, None, ALU.add).then_inc(rstd_steps, 1)
                pool.wait_ge(rstd_steps, bn * 8 + c * 2 + 1)
                nc.gpsimd.tensor_tensor(rstd[:, blocks], veps[:, blocks], minus_half[:, blocks], ALU.pow).then_inc(rstd_steps, 1)

            def add_biases(bn, par, c):
                pool.wait_ge(x_landed[par], bn * 8 + (8 if par else 16))
                for i in (2 * c, 2 * c + 1):
                    last = nc.gpsimd.tensor_tensor(x[par][:, i, :], x[par][:, i, :], bo[:], ALU.add)
                last.then_inc(xb_ready, 1)

            def mask_bank(b, g, r, a):
                wait_alone(pool, exped, b * (2 * SLOTS) + g * NHALF + 2 * r + a + 1)
                tile_ = pt[(2 * r + a) % PT_RING]
                if REGIONS[r][0] == "A":
                    n, blocks = 1, tile_[:, 0:P]
                elif REGIONS[r][0] == "B":
                    n, blocks = 2, tile_[:, :].rearrange("p (c t) -> p c t", t=P)[:, 0:4:3, :]
                else:
                    n, blocks = 2, tile_[:, :].rearrange("p (h w) -> p h w", h=2)[:, :, 0:P]
                nc.gpsimd.affine_select(out=blocks, in_=blocks, compare_op=ALU.is_ge, fill=0.0, base=0, pattern=[[0, n], [1, P]],
                                        channel_multiplier=-1).then_inc(masked, 1)

            def scale_heads(b, hh):
                pool.wait_ge(sc_landed, (b * QUADS + 2 * hh + 2) * 32)
                for n in range(2):
                    for half in range(2):
                        pool.wait_ge(halves_landed[half], (b * QUADS + 2 * hh + 2) * 80)
                    cols = slice(n * HALF, (n + 1) * HALF)
                    last = nc.gpsimd.tensor_tensor(oc[:, hh, cols], oc[:, hh, cols], sc[:, cols], ALU.mult)
                last.then_inc(attn_ready, 1)

            def first():
                nc.gpsimd.memset(minus_half[:], -0.5)
                nc.gpsimd.memset(identf[:], 0.0)
                nc.gpsimd.memset(identb[:], 0.0)
                nc.gpsimd.memset(maskb[:], 0.0).then_inc(pool_steps, 1)
                pool.wait_ge(pool_steps, 1)
                for m in (identf, identb):
                    nc.gpsimd.affine_select(out=m[:], in_=m[:], compare_op=ALU.not_equal, fill=1.0, base=0, pattern=[[-1, P]], channel_multiplier=1)
                nc.gpsimd.affine_select(out=maskb[:], in_=maskb[:], compare_op=ALU.is_ge, fill=MASKED, base=0, pattern=[[-1, P]],
                                        channel_multiplier=1).then_inc(ident_ready, 1)
                for c in range(4):
                    inverse_deviation(0, c)
                pool.wait_ge(rstd_steps, 8)
                for g in (1, 2, 3):
                    last = nc.gpsimd.memset(ks[g][STACK:MROWS, :, :], 1.0)
                last.then_inc(pool_steps, 1)
                pool.wait_ge(pool_steps, 2)
                pool.wait_ge(weights_landed, 16 * 7)
                nc.gpsimd.tensor_tensor(bo[:], bo[:], bb[:], ALU.add).then_inc(bias_ready, 1)
                pool.wait_ge(bias_ready, 1)
                for c in range(4):
                    add_biases(0, 0, c)

            def period(b, par):
                for s in range(SLOTS):
                    g, r = divmod(s, NREG)
                    if r in MASK_REGIONS:
                        for a in range(2):
                            mask_bank(b, g, r, a)
                    if r == 10 and g == 2:
                        scale_heads(b, 0)
                    if r == 10 and g == 0 and not is_zero(b):
                        scale_heads(b - 1, 1)
                    for kind, idx in tasks_at(b, s):
                        if kind == "stats":
                            inverse_deviation(b + 1, idx)
                        elif kind == "norm":
                            normalise(pool, nc.gpsimd, b + 1, idx)
                        elif kind == "bias":
                            add_biases(b + 1, 1 - par, idx)
                        elif kind == "rotated":
                            rotated(pool, nc.gpsimd, b + 1, idx)
                        elif kind == "left0":
                            left_over(pool, nc.gpsimd, b + 1, idx, 0)
                        elif kind == "left1":
                            left_over(pool, nc.gpsimd, b + 1, idx, 1)

            def end():
                scale_heads(B - 1, 1)

            run_periods(pool, first, period, end)


_INS = ["x_in", "wqk_in", "bqk_in", "wv_in", "bv_in", "base_in", "wout_in", "lora_in", "bo_in", "bb_in", "cos_in", "sin_in"]


def kernel(**inputs):
    import numpy as np
    import concourse.bacc as bacc
    from concourse.bass_utils import run_bass_kernel_spmd

    def rows_of(a):
        return a.reshape(KD, P, -1).transpose(1, 0, 2)

    w = np.asarray(inputs["L0_attn_w_qkv"])
    b = np.asarray(inputs["L0_attn_b_qkv"])
    w_pairs = w[:2 * D].reshape(2, H, DH // 2, 2, D).transpose(0, 3, 1, 2, 4).reshape(4, P, D)
    b_pairs = b[:2 * D].reshape(2, H, DH // 2, 2).transpose(0, 3, 1, 2).reshape(4, P)
    inv_freq = (1.0 / np.float32(10000.0) ** (np.arange(0, DH, 2, dtype=np.float32) / np.float32(DH))).astype(np.float32)
    angle = np.tile(inv_freq, H)[:, None] * np.arange(T, dtype=np.float32)[None, :]
    wv = np.concatenate([w[2 * D:].T, np.asarray(inputs["L0_ffn_lora_A"]), np.asarray(inputs["L0_ffn_router_w"]).T], axis=1)
    bv = np.concatenate([b[2 * D:], np.zeros(R, np.float32), np.asarray(inputs["L0_ffn_router_b"])])
    lora_b = np.asarray(inputs["L0_ffn_lora_B"]).reshape(E * R, D)
    arrays = {
        "x_in": np.asarray(inputs["L0_attn_x"]),
        "wqk_in": w_pairs.reshape(4, P, KD, P).transpose(3, 2, 0, 1),
        "bqk_in": b_pairs.T,
        "wv_in": rows_of(wv),
        "bv_in": np.broadcast_to(bv, (P, D + NML)),
        "base_in": rows_of(np.asarray(inputs["L0_ffn_base_w"]).T),
        "wout_in": rows_of(np.asarray(inputs["L0_attn_w_out"]).T),
        "lora_in": np.stack([np.concatenate([lora_b, np.zeros_like(lora_b)]), np.concatenate([np.zeros_like(lora_b), lora_b])], axis=1),
        "bo_in": np.broadcast_to(np.asarray(inputs["L0_attn_b_out"]), (P, D)),
        "bb_in": np.broadcast_to(np.asarray(inputs["L0_ffn_base_b"]), (P, D)),
        "cos_in": np.cos(angle).astype(np.float32),
        "sin_in": np.sin(angle).astype(np.float32),
    }
    nc = bacc.Bacc("TRN2", target_bir_lowering=False, num_devices=1)
    given, args = {}, []
    for name in _INS:
        a = np.ascontiguousarray(arrays[name])
        given[f"{name}_dram"] = a
        args.append(nc.dram_tensor(f"{name}_dram", a.shape, mybir.dt.from_np(a.dtype), kind="ExternalInput").ap())
    args.append(nc.dram_tensor("out_dram", (B, T, D), mybir.dt.float32, kind="ExternalOutput").ap())
    attention_ffn_block(nc, *args)
    r = run_bass_kernel_spmd(nc, [given], core_ids=[0])
    return r.results[0]["out_dram"]
```
